# Optimizing a Trainium2 kernel written in Bass

```python
import numpy as np
import jax
import jax.numpy as jnp

def _softmax(x, axis=-1):
    return jax.nn.softmax(x, axis=axis)

def _gelu(x):
    return jax.nn.gelu(x, approximate=True)

def _silu(x):
    return jax.nn.silu(x)

def _sigmoid(x):
    return jax.nn.sigmoid(x)

def _layernorm(x, axis=-1, eps=1e-05):
    m = jnp.mean(x, axis=axis, keepdims=True)
    v = jnp.var(x, axis=axis, keepdims=True)
    return (x - m) / jnp.sqrt(v + eps)

def _scatter_add(tgt, idx, src, axis=0):
    return tgt.at[idx].add(src)

def _segment_sum(src, seg, n):
    return jax.ops.segment_sum(src, seg, n)
kernel_name = 'mk_gnn_resnorm_d1_gnn_r32_35d9a3'

def setup_inputs(seed: int=0):
    np.random.seed(seed)
    _w = jnp.asarray

    def _rec_inputs():
        import jax
        import jax.numpy as jnp
        _gk = jax.random.key(seed)
        x = -0.0003713 + 1 * jax.random.normal(jax.random.fold_in(_gk, 1), (3125, 128), jnp.float32)
        _s = jax.random.randint(jax.random.fold_in(_gk, 2), (25000,), 0, 3125, jnp.int32)
        _d = jax.random.randint(jax.random.fold_in(_gk, 3), (25000,), 0, 3125, jnp.int32)
        _loop = jnp.arange(3125, dtype=jnp.int32)
        src = jnp.concatenate([_s, _d, _loop])
        dst = jnp.concatenate([_d, _s, _loop])
        _o = jnp.argsort(dst, stable=True)
        src = src[_o]
        dst = dst[_o]
        edge_attr_64 = 0.000102155 + 1.00015 * jax.random.normal(jax.random.fold_in(_gk, 11), (53125, 64), jnp.float32)
        return (x, src, dst, edge_attr_64)
    x, src, dst, edge_attr_64 = _rec_inputs()

    def _L0_gnn_setup():
        import jax, jax.numpy as jnp
        import numpy as np
        D_NODE = 128
        D_EDGE = 64
        N_NODES = 3125
        N_EDGES = 15625
        key = jax.random.key(seed)
        ks = jax.random.split(key, 12)

        def lin(k, fan_in, fan_out):
            bound = 1.0 / np.sqrt(fan_in)
            kw, kb = jax.random.split(k)
            W = jax.random.uniform(kw, (fan_in, fan_out), jnp.float32, -bound, bound)
            b = jax.random.uniform(kb, (fan_out,), jnp.float32, -bound, bound)
            return (W, b)
        node_features = jax.random.normal(ks[0], (N_NODES, D_NODE), jnp.float32)
        edge_index = jax.random.randint(ks[1], (2, N_EDGES), 0, N_NODES, jnp.int64 if jax.config.jax_enable_x64 else jnp.int32)
        edge_features = jax.random.normal(ks[2], (N_EDGES, D_EDGE), jnp.float32)
        W1, b1 = lin(ks[3], 2 * D_NODE + D_EDGE, D_NODE)
        W2, b2 = lin(ks[4], D_NODE, D_NODE)
        Wg, bg = lin(ks[5], 2 * D_NODE, D_NODE)
        Wt, bt = lin(ks[6], 2 * D_NODE, D_NODE)
        gamma = jnp.ones((D_NODE,), jnp.float32)
        beta = jnp.zeros((D_NODE,), jnp.float32)
        return {'node_features': node_features, 'edge_features': edge_features, 'W1': W1, 'b1': b1, 'W2': W2, 'b2': b2, 'Wg': Wg, 'bg': bg, 'Wt': Wt, 'bt': bt, 'gamma': gamma, 'beta': beta, 'edge_index': edge_index}
    _L0_gnn_all = _L0_gnn_setup()
    _L0_gnn_in = {k: v for k, v in _L0_gnn_all.items() if k in ('W1', 'b1', 'W2', 'b2', 'Wg', 'bg', 'Wt', 'bt', 'gamma', 'beta')}
    del _L0_gnn_all
    return {'x': x, 'src': src, 'dst': dst, 'edge_attr_64': edge_attr_64, 'L0_gnn_W1': _L0_gnn_in['W1'], 'L0_gnn_b1': _L0_gnn_in['b1'], 'L0_gnn_W2': _L0_gnn_in['W2'], 'L0_gnn_b2': _L0_gnn_in['b2'], 'L0_gnn_Wg': _L0_gnn_in['Wg'], 'L0_gnn_bg': _L0_gnn_in['bg'], 'L0_gnn_Wt': _L0_gnn_in['Wt'], 'L0_gnn_bt': _L0_gnn_in['bt'], 'L0_gnn_gamma': _L0_gnn_in['gamma'], 'L0_gnn_beta': _L0_gnn_in['beta']}

def reference(x, src, dst, edge_attr_64, L0_gnn_W1, L0_gnn_b1, L0_gnn_W2, L0_gnn_b2, L0_gnn_Wg, L0_gnn_bg, L0_gnn_Wt, L0_gnn_bt, L0_gnn_gamma, L0_gnn_beta):
    import jax
    import jax.numpy as jnp

    def _L0_gnn_ref(node_features, edge_features, W1, b1, W2, b2, Wg, bg, Wt, bt, gamma, beta, edge_index):
        import jax, jax.numpy as jnp
        import numpy as np
        D_NODE = 128
        D_EDGE = 64
        N_NODES = 3125
        N_EDGES = 15625
        num_nodes = node_features.shape[0]
        src, dst = (edge_index[0], edge_index[1])
        h_src = node_features[src]
        h_dst = node_features[dst]
        msg_in = jnp.concatenate([h_src, h_dst, edge_features], axis=-1)
        messages = jax.nn.silu(msg_in @ W1 + b1) @ W2 + b2
        aggregated = jax.ops.segment_sum(messages, dst, num_segments=num_nodes)
        count = jax.ops.segment_sum(jnp.ones((dst.shape[0],), messages.dtype), dst, num_segments=num_nodes)
        aggregated = aggregated / jnp.clip(count, 1.0)[:, None]
        gate_in = jnp.concatenate([node_features, aggregated], axis=-1)
        gate = jax.nn.sigmoid(gate_in @ Wg + bg)
        transform = jnp.tanh(gate_in @ Wt + bt)
        updated = gate * node_features + (1.0 - gate) * transform
        mu = jnp.mean(updated, axis=-1, keepdims=True)
        var = jnp.var(updated, axis=-1, keepdims=True)
        normed = (updated - mu) * jax.lax.rsqrt(var + 1e-05)
        return normed * gamma + beta
    edge_index = jnp.stack([src, dst])
    x = _layernorm(x + _L0_gnn_ref(x, edge_attr_64, L0_gnn_W1, L0_gnn_b1, L0_gnn_W2, L0_gnn_b2, L0_gnn_Wg, L0_gnn_bg, L0_gnn_Wt, L0_gnn_bt, L0_gnn_gamma, L0_gnn_beta, edge_index), axis=-1)
    return x

_drawn_inputs = setup_inputs


def setup_inputs(seed=0):
    import zlib

    import numpy as np

    out = dict(_drawn_inputs(seed))
    spreads = {'L0_gnn_gamma': (1.0, 0.2), 'L0_gnn_beta': (0.0, 0.1)}
    factors = {'edge_attr_64': 8.0,
     'L0_gnn_b1': 26.601,
     'L0_gnn_b2': 5.31,
     'L0_gnn_bg': 6.417,
     'L0_gnn_bt': 3.835}
    for name, (base, spread) in spreads.items():
        noise = np.random.default_rng([zlib.crc32(name.encode()), seed]).standard_normal(out[name].shape)
        drawn = base * np.exp(spread * noise) if base else spread * noise
        out[name] = jnp.asarray(drawn.astype(out[name].dtype))
    for name, factor in factors.items():
        out[name] = (out[name] * factor).astype(out[name].dtype)
    return out
```

```python
import math
from contextlib import ExitStack

import numpy as np
import concourse.bass as bass
from concourse import mybir

ALU = mybir.AluOpType
ACT = mybir.ActivationFunctionType
AX = mybir.AxisListType
F32 = mybir.dt.float32
I32 = mybir.dt.int32

P = 128
D = 128
DE = 64
WIN = 64
EPS = 1e-5

GROUPS = (4, 4, 3, 3, 3)
OFFS = (0, 4, 8, 11, 14)
NG = len(GROUPS)
TILES = sum(GROUPS)
KMAX = max(GROUPS)
BPI = 8
AHEAD = 3


def shapes(n_nodes, n_edges):
    blocks = -(-n_nodes // P)
    tiles = -(-n_edges // P)
    iters = min(tiles // TILES, blocks - 1)
    last = []
    left = tiles - iters * TILES
    off = 0
    while left > 0:
        k = min(KMAX, left)
        last.append((off, k))
        off += k
        left -= k
    assert len(last) <= NG and iters >= 4
    return blocks, tiles, iters, last


def gnn_kernel(nc, x, xT, src_pt, dst_pt, dst_flat, base_tab, open_tab, efT,
               W1, b1, W2T, b2, Wg, bg, Wt, bt, gamma, beta, out):
    N = out.shape[0]
    NP = x.shape[0]
    NB, NT, ITERS, LAST = shapes(N, src_pt.shape[1] * P)
    assert NP == NB * P and D == P
    NBASE = base_tab.shape[1]
    ROWS_LAST = N - (NB - 1) * P
    RING = 3

    def before(j):
        for back in range(1, NG + 1):
            if (j - back) % NG % RING == j % RING:
                return back

    with ExitStack() as ctx:
        def sb(name, shape, dt=F32):
            return ctx.enter_context(nc.sbuf_tensor(name, shape, dt))

        def ps(name, shape):
            return ctx.enter_context(nc.psum_tensor(name, shape, F32))

        def sem(name):
            return ctx.enter_context(nc.semaphore(name))

        psrc_d = nc.dram_tensor("psrc_d", [NP, D], F32).ap()
        pdst_d = nc.dram_tensor("pdst_d", [NP, D], F32).ap()

        xT_all = sb("xT_all", [P, NP])
        x_all = sb("x_all", [P, NB, D])
        w1s = sb("w1s", [P, D])
        w1d = sb("w1d", [P, D])
        w2T = sb("w2T", [P, D])
        wx = sb("wx", [P, 2 * D])
        wa = sb("wa", [P, 2 * D])
        w2a = sb("w2a", [P, 2 * D])
        b2c = sb("b2c", [P, 1])
        b2a = sb("b2a", [1, 2 * D])
        bgt = sb("bgt", [1, 2 * D])
        b1_bc = sb("b1_bc", [P, D])
        gamma_bc = sb("gamma_bc", [P, D])
        beta_bc = sb("beta_bc", [P, D])
        ones = sb("ones", [P, P])
        iota_i = sb("iota_i", [P, P], I32)
        iota_f = sb("iota_f", [P, P])
        node_i = sb("node_i", [P, 1], I32)
        node_f = sb("node_f", [P, 1])
        src_i = sb("src_i", [P, NT], I32)
        dst_i = sb("dst_i", [P, NT], I32)
        base_i = sb("base_i", [P, NBASE], I32)
        open_i = sb("open_i", [P, NBASE], I32)
        base_f = sb("base_f", [P, NBASE])
        base_col = sb("base_col", [P, NBASE])
        slack = sb("slack", [P, NBASE])
        rel = sb("rel", [P, NT])
        dst_f = sb("dst_f", [P, NT])
        red = sb("red", [P, 4])
        bad = sb("bad", [P, 4])
        flag = sb("flag", [1, 1], I32)
        aggcnt = sb("aggcnt", [P, 2, NP])
        pst = sb("pst", [P, 2, NB, D])

        idx = sb("idx", [P, NG, KMAX], I32)
        lhs = sb("lhs", [P, NG, KMAX * P])
        dstb = sb("dstb", [P, NG, KMAX * P], I32)
        win = sb("win", [P, NG, D])
        gath = sb("gath", [P, NG, KMAX, D])
        onehot = sb("onehot", [P, NG, KMAX, WIN])
        h = sb("h", [P, RING, KMAX, D])

        xT_blk = sb("xT_blk", [P, P])
        ablk = sb("ablk", [P, 2, P])
        xg = sb("xg", [P, 2 * D])
        gt = sb("gt", [P, 2 * D])
        th = sb("th", [P, 2 * D])
        rcp = sb("rcp", [P, 2])
        diff = sb("diff", [P, D])
        mix = sb("mix", [P, D])
        upd = sb("upd", [P, D])
        xb = sb("xb", [P, D])
        nrm = sb("nrm", [P, D])
        ysum = sb("ysum", [P, D])
        ynew = sb("ynew", [P, D])
        stats = sb("stats", [P, 6])
        mv = sb("mv", [P, 2])
        nhv = sb("nhv", [P, 1])
        yi = sb("yi", [P, 2], I32)
        nt = sb("nt", [P, 4])
        oblk = sb("oblk", [P, D])

        sidx = sb("sidx", [P, 2], I32)
        sef = sb("sef", [DE, P])
        sgath = sb("sgath", [P, 2, D])
        sh = sb("sh", [P, D])
        shift = sb("shift", [P, 1])
        soh = sb("soh", [P, P])

        pre = [ps(f"pre{r}", [P, KMAX * D]) for r in range(RING)]
        pagg = [ps(f"pagg{r}", [P, 512]) for r in range(2)]
        pnx = ps("pnx", [P, 512])
        pna = ps("pna", [P, 512])
        pmisc = ps("pmisc", [P, 512])
        banks = pre + pagg + [pnx, pna]

        XCH = 4
        NCH = -(-NB // XCH)
        w1_in = sem("w1_in")
        xT_in = [sem(f"xT_in{c}") for c in range(NCH)]
        tab_in = sem("tab_in")
        wgt_in = sem("wgt_in")
        bc_in = sem("bc_in")
        src_in = sem("src_in")
        win_in = sem("win_in")
        x_in = sem("x_in")
        ones_ready = sem("ones_ready")
        iota_ready = sem("iota_ready")
        tab_mm = sem("tab_mm")
        psrc_sb = sem("psrc_sb")
        pdst_sb = sem("pdst_sb")
        psrc_out = sem("psrc_out")
        pdst_out = sem("pdst_out")
        prep = sem("prep")
        bad_ready = sem("bad_ready")
        bad_mm = sem("bad_mm")
        flag_ready = sem("flag_ready")
        half = sem("half")
        fold_mm = sem("fold_mm")
        fold_ready = sem("fold_ready")
        slot_in = [sem(f"slot_in{j}") for j in range(NG)]
        gath_in = [sem(f"gath_in{j}") for j in range(NG)]
        idx_ready = sem("idx_ready")
        ohT_done = sem("ohT_done")
        oh_ready = sem("oh_ready")
        pre_done = sem("pre_done")
        sum_done = sem("sum_done")
        h_ready = sem("h_ready")
        agg_done = sem("agg_done")
        added = sem("added")
        passed = sem("passed")
        xT_blk_in = sem("xT_blk_in")
        ablk_ready = sem("ablk_ready")
        node_mm = sem("node_mm")
        xg_ready = sem("xg_ready")
        gt_ready = sem("gt_ready")
        th_ready = sem("th_ready")
        upd_ready = sem("upd_ready")
        chain = sem("chain")
        out_ready = sem("out_ready")
        out_done = sem("out_done")
        g_idx_half = sem("g_idx_half")
        g_idx = sem("g_idx")
        g_ef = sem("g_ef")
        g_gath = sem("g_gath")
        g_pre = sem("g_pre")
        g_sum0 = sem("g_sum0")
        g_sum = sem("g_sum")
        g_h = sem("g_h")
        g_shift = sem("g_shift")
        g_oh = sem("g_oh")
        g_mm = sem("g_mm")
        g_added = sem("g_added")

        block = ctx.enter_context(nc.Block())

        def groups_of(i):
            if isinstance(i, int) and i == ITERS:
                return [(j, off, k) for j, (off, k) in enumerate(LAST)]
            return list(zip(range(NG), OFFS, GROUPS))

        def take_waits(eng):
            eng.sem_inc(passed, 1)

        def run_iterations(eng, body):
            for i in range(3):
                body(i)
            with eng.Fori(3, ITERS) as i:
                body(i)
            body(ITERS)

        def load_base(eng, i, j):
            return eng.value_load(base_i[0:1, bass.ds(i * BPI + j, 1)], min_val=0, max_val=N)

        def loop_blocks(eng, stage):
            stage(0)
            with eng.Fori(1, NB - 1) as b:
                stage(b)
            stage(NB - 1)

        @block.sync
        def _(sp):
            sp.dma_start(w1s[:, :], W1[0:D, :]).then_inc(w1_in, 16)
            sp.dma_start(w1d[:, :], W1[D:2 * D, :]).then_inc(w1_in, 16)
            for c in range(NCH):
                lo, hi = c * XCH * P, min((c + 1) * XCH, NB) * P
                sp.dma_start(xT_all[:, lo:hi], xT[:, lo:hi]).then_inc(xT_in[c], 16)
            sp.dma_start(win[0:DE, :, :], W1[2 * D:2 * D + DE, :].rearrange("k (a n) -> k a n", a=1)
                         .to_broadcast([DE, NG, D])).then_inc(win_in, 16)
            sp.dma_start(x_all[:, :, :], x.rearrange("(b p) f -> p b f", p=P)).then_inc(x_in, 16)
            for t, (d, ready, sent) in enumerate(((psrc_d, psrc_sb, psrc_out), (pdst_d, pdst_sb, pdst_out))):
                dv = d.rearrange("(b p) f -> p b f", p=P)
                for c in range(NCH):
                    lo, hi = c * XCH, min((c + 1) * XCH, NB)
                    sp.wait_ge(ready, c + 1)
                    sp.dma_start(dv[:, lo:hi, :], pst[:, t, lo:hi, :]).then_inc(sent, 16)
            sp.wait_ge(pdst_out, 16 * NCH)
            sp.wait_ge(win_in, 16)
            sp.wait_ge(flag_ready, 1)
            bad_v = sp.value_load(flag[0:1, 0:1], min_val=0, max_val=3 * P)

            def xT_load(b):
                if not (isinstance(b, int) and b == 0):
                    sp.wait_ge(node_mm, b)
                sp.dma_start(xT_blk[:, :], xT[:, bass.ds(b * P, P)]).then_inc(xT_blk_in, 16)

            def out_store(b):
                sp.wait_ge(out_ready, b + 1)
                if isinstance(b, int) and b == NB - 1:
                    sp.dma_start(out[b * P:N, :], oblk[0:ROWS_LAST, :]).then_inc(out_done, 16)
                else:
                    sp.dma_start(out[bass.ds(b * P, P), :], oblk[:, :]).then_inc(out_done, 16)

            def body(i):
                for j, off, k in groups_of(i):
                    if not (isinstance(i, int) and i == 0):
                        sp.wait_ge(pre_done, i * NG + (j - NG + 1))
                    e0 = (i * TILES + off) * P
                    base = load_base(sp, i, j)
                    sp.dma_start(dstb[DE:P, j, 0:k * P],
                                 dst_flat[0:1, bass.ds(e0, k * P)].to_broadcast([WIN, k * P])).then_inc(slot_in[j], 16)
                    sp.dma_start(lhs[0:DE, j, 0:k * P], efT[:, bass.ds(e0, k * P)]).then_inc(slot_in[j], 16)
                    sp.dma_start(win[DE:P, j, :], pdst_d[bass.ds(base, WIN), :]).then_inc(slot_in[j], 16)
                    if j == 1 and not (isinstance(i, int) and i < 2):
                        xT_load(i - 2)
                if not (isinstance(i, int) and (i < 3 or i == ITERS)):
                    out_store(i - 3)

            with sp.If(bad_v == 0):
                run_iterations(sp, body)
                out_store(ITERS - 3)
                xT_load(ITERS - 1)
                out_store(ITERS - 2)
                xT_load(NB - 1)
                out_store(ITERS - 1)
                out_store(NB - 1)
            with sp.Else():
                def load_tile(t):
                    if not isinstance(t, int):
                        sp.wait_ge(g_pre, t)
                    sp.dma_start(sef[:, :], efT[:, bass.ds(t * P, P)]).then_inc(g_ef, 16)
                load_tile(0)
                with sp.Fori(1, NT) as t:
                    load_tile(t)

                def stage(b):
                    xT_load(b)
                    out_store(b)
                loop_blocks(sp, stage)
            sp.wait_ge(out_done, 16 * NB)

        @block.gpsimd
        def _(pool):
            nc.gpsimd.iota(iota_i[:, :], pattern=[[1, P]], base=0, channel_multiplier=0).then_inc(iota_ready, 1)
            nc.gpsimd.iota(node_i[:, :], pattern=[[0, 1]], base=-WIN, channel_multiplier=1).then_inc(iota_ready, 1)
            pool.wait_ge(flag_ready, 1)
            bad_v = pool.value_load(flag[0:1, 0:1], min_val=0, max_val=3 * P)

            def body(i):
                for j, off, k in groups_of(i):
                    pool.wait_ge(idx_ready, i * NG + (j + 1))
                    if not (isinstance(i, int) and i == 0):
                        pool.wait_ge(sum_done, i * NG + (j - NG + 1))
                        take_waits(pool)
                    for c in range(k):
                        nc.gpsimd.indirect_dma_start(
                            out=gath[:, j, c, :], out_offset=None, in_=psrc_d,
                            in_offset=bass.IndirectOffsetOnAxis(ap=idx[:, j, c:c + 1], axis=0)).then_inc(gath_in[j], 16)

            pool.wait_ge(psrc_out, 16 * NCH)
            with pool.If(bad_v == 0):
                run_iterations(pool, body)
            with pool.Else():
                pool.wait_ge(pdst_out, 16 * NCH)

                def gather_tile(t):
                    pool.wait_ge(g_idx, t + 1)
                    if not isinstance(t, int):
                        pool.wait_ge(g_sum, t)
                        take_waits(pool)
                    for c, table in enumerate((psrc_d, pdst_d)):
                        nc.gpsimd.indirect_dma_start(
                            out=sgath[:, c, :], out_offset=None, in_=table,
                            in_offset=bass.IndirectOffsetOnAxis(ap=sidx[:, c:c + 1], axis=0)).then_inc(g_gath, 16)
                gather_tile(0)
                with pool.Fori(1, NT) as t:
                    gather_tile(t)

        @block.scalar
        def _(act):
            act.dma_start(src_i[:, :], src_pt).then_inc(src_in, 16)
            act.dma_start(dst_i[:, :], dst_pt).then_inc(tab_in, 16)
            act.dma_start(base_i[:, :], base_tab.to_broadcast([P, NBASE])).then_inc(tab_in, 16)
            act.dma_start(open_i[:, :], open_tab.to_broadcast([P, NBASE])).then_inc(tab_in, 16)
            act.dma_start(b1_bc[:, :], b1.to_broadcast([P, D])).then_inc(bc_in, 16)
            act.dma_start(gamma_bc[:, :], gamma.to_broadcast([P, D])).then_inc(bc_in, 16)
            act.dma_start(beta_bc[:, :], beta.to_broadcast([P, D])).then_inc(bc_in, 16)
            for dst_ap, src_ap in ((wx[:, 0:D], Wg[0:D, :]), (wx[:, D:2 * D], Wt[0:D, :]),
                                   (wa[:, 0:D], Wg[D:2 * D, :]), (wa[:, D:2 * D], Wt[D:2 * D, :]),
                                   (bgt[:, 0:D], bg), (bgt[:, D:2 * D], bt),
                                   (w2T[:, :], W2T), (b2c[:, :], b2)):
                act.dma_start(dst_ap, src_ap).then_inc(wgt_in, 16)
            act.wait_ge(ones_ready, 1)
            nc.scalar.activation(sh[:, 0:1], ones[:, 0:1], ACT.Silu).then_inc(half, 1)
            for c in range(0, NCH):
                lo, hi = c * XCH, min((c + 1) * XCH, NB)
                act.wait_ge(tab_mm, c + 1)
                nc.scalar.activation(pst[:, 0, lo:hi, :], banks[c % len(banks)][:, 0:(hi - lo) * D]
                                     .rearrange("p (b f) -> p b f", f=D), ACT.Copy).then_inc(psrc_sb, 1)
            act.wait_ge(wgt_in, 16 * 8)
            for w in (wx, wa, bgt):
                nc.scalar.activation(w[:, 0:D], w[:, 0:D], ACT.Copy, scale=0.5).then_inc(half, 1)
            act.wait_ge(src_in, 16)
            for j in range(NG):
                nc.scalar.activation(idx[:, j, 0:GROUPS[j]], src_i[:, OFFS[j]:OFFS[j] + GROUPS[j]],
                                     ACT.Copy).then_inc(idx_ready, 1)
            act.wait_ge(fold_mm, 1)
            nc.scalar.activation(w2a[:, :], pmisc[:, 0:2 * D], ACT.Copy).then_inc(fold_ready, 1)
            nc.scalar.activation(b2a[:, :], pmisc[0:1, 2 * D:4 * D], ACT.Copy).then_inc(fold_ready, 1)

            act.wait_ge(flag_ready, 1)
            bad_v = act.value_load(flag[0:1, 0:1], min_val=0, max_val=3 * P)

            def first(b):
                return isinstance(b, int) and b == 0

            def stage_copy(b):
                if not first(b):
                    act.wait_ge(node_mm, b)
                nc.scalar.activation(ablk[:, :, :], aggcnt[:, :, bass.ds(b * P, P)], ACT.Copy).then_inc(ablk_ready, 1)

            def stage_xg(b):
                act.wait_ge(node_mm, b + 1)
                if not first(b):
                    act.wait_ge(gt_ready, b)
                nc.scalar.activation(xg[:, :], pnx[:, 0:2 * D], ACT.Copy).then_inc(xg_ready, 1)

            def stage_tanh(b):
                act.wait_ge(gt_ready, b + 1)
                if not first(b):
                    act.wait_ge(upd_ready, b)
                nc.scalar.activation(th[:, :], gt[:, :], ACT.Tanh).then_inc(th_ready, 1)

            def silu(i, j, off, k):
                act.wait_ge(sum_done, i * NG + (j + 1))
                if not (isinstance(i, int) and i * NG + j < before(j)):
                    act.wait_ge(agg_done, i * NG + (j + 1 - before(j)))
                nc.scalar.activation(h[:, j % RING, 0:k, :], pre[j % RING][:, 0:k * D]
                                     .rearrange("p (c f) -> p c f", f=D), ACT.Silu).then_inc(h_ready, 1)

            def next_idx(i, j):
                nxt = groups_of(i + 1) if isinstance(i, int) else groups_of(None)
                if j < len(nxt):
                    _, off, k = nxt[j]
                    nc.scalar.activation(idx[:, j, 0:k], src_i[:, bass.ds(i * TILES + (TILES + off), k)],
                                         ACT.Copy).then_inc(idx_ready, 1)

            def body(i, to_last=False):
                for j, off, k in groups_of(i):
                    if j == NG - 1 and not first(i):
                        act.wait_ge(added, i * NG + AHEAD)
                        stage_copy(i - 1)
                    silu(i, j, off, k)
                    if to_last:
                        if j < len(LAST):
                            _, o, kk = groups_of(ITERS)[j]
                            nc.scalar.activation(idx[:, j, 0:kk], src_i[:, ITERS * TILES + o:ITERS * TILES + o + kk],
                                                 ACT.Copy).then_inc(idx_ready, 1)
                    elif not (isinstance(i, int) and i == ITERS):
                        next_idx(i, j)
                    if not (isinstance(i, int) and i < 2):
                        if j == 0:
                            stage_xg(i - 2)
                        if j == 1:
                            stage_tanh(i - 2)

            with act.If(bad_v == 0):
                for i in range(3):
                    body(i)
                with act.Fori(3, ITERS - 1) as i:
                    body(i)
                body(ITERS - 1, to_last=True)
                body(ITERS)
                act.wait_ge(added, ITERS * NG + len(LAST))
                for b in range(ITERS - 1, NB):
                    stage_copy(b)
                    stage_xg(b)
                    stage_tanh(b)
            with act.Else():
                def idx_tile(t):
                    if not isinstance(t, int):
                        act.wait_ge(g_gath, 32 * t)
                    nc.scalar.activation(sidx[:, 0:1], src_i[:, bass.ds(t, 1)], ACT.Copy).then_inc(g_idx_half, 1)
                    nc.scalar.activation(sidx[:, 1:2], dst_i[:, bass.ds(t, 1)], ACT.Copy).then_inc(g_idx, 1)
                    act.wait_ge(g_sum, t + 1)
                    if not isinstance(t, int):
                        act.wait_ge(g_mm, t * NB)
                    nc.scalar.activation(sh[:, :], pre[1][:, 0:D], ACT.Silu).then_inc(g_h, 1)
                idx_tile(0)
                with act.Fori(1, NT) as t:
                    idx_tile(t)
                act.wait_ge(g_added, NT * NB)

                def stage(b):
                    stage_copy(b)
                    stage_xg(b)
                    stage_tanh(b)
                loop_blocks(act, stage)

        @block.tensor
        def _(pe):
            pe.wait_ge(w1_in, 32)
            n = 0
            for w in (w1s, w1d):
                for c in range(NCH):
                    lo, hi = c * XCH, min((c + 1) * XCH, NB)
                    if w is w1s:
                        pe.wait_ge(xT_in[c], 16)
                    if n >= len(banks):
                        m = n - len(banks)
                        pe.wait_ge(*((psrc_sb, m + 1) if m < NCH else (pdst_sb, m - NCH + 1)))
                    for b in range(lo, hi):
                        mm = nc.tensor.matmul(banks[n % len(banks)][:, (b - lo) * D:(b - lo + 1) * D],
                                              lhsT=xT_all[:, b * P:(b + 1) * P], rhs=w[:, :], start=True, stop=True)
                    mm.then_inc(tab_mm, 1)
                    n += 1
            pe.wait_ge(half, 4)
            nc.tensor.matmul(pmisc[:, 0:2 * D], lhsT=w2T[:, :], rhs=wa[:, :], start=True, stop=True)
            nc.tensor.matmul(pmisc[0:1, 2 * D:4 * D], lhsT=b2c[:, :], rhs=wa[:, :],
                             start=True, stop=True).then_inc(fold_mm, 1)
            pe.wait_ge(bad_ready, 1)
            pe.wait_ge(fold_ready, 2)
            nc.tensor.matmul(pmisc[0:1, 0:1], lhsT=bad[:, 3:4], rhs=ones[:, 0:1], start=True, stop=True).then_inc(bad_mm, 1)
            pe.wait_ge(flag_ready, 1)
            bad_v = pe.value_load(flag[0:1, 0:1], min_val=0, max_val=3 * P)

            def first(b):
                return isinstance(b, int) and b == 0

            def node_products(b):
                pe.wait_ge(ablk_ready, b + 1)
                pe.wait_ge(xT_blk_in, b * 16 + 16)
                if not first(b):
                    pe.wait_ge(xg_ready, b)
                    pe.wait_ge(gt_ready, b)
                nc.tensor.matmul(pnx[:, 0:2 * D], lhsT=xT_blk[:, :], rhs=wx[:, :], start=True, stop=False)
                nc.tensor.matmul(pnx[:, 0:2 * D], lhsT=ones[0:1, :], rhs=bgt[:, :], start=False, stop=True)
                nc.tensor.matmul(pna[:, 0:2 * D], lhsT=ablk[:, 0, :], rhs=w2a[:, :], start=True, stop=False)
                nc.tensor.matmul(pna[:, 0:2 * D], lhsT=ablk[0:1, 1, :], rhs=b2a[:, :], start=False, stop=True)
                nc.tensor.matmul(pna[:, 2 * D:2 * D + 1], lhsT=ablk[0:1, 1, :], rhs=ones[0:1, 0:1],
                                 start=True, stop=True).then_inc(node_mm, 1)

            def pre_products(i, j, k):
                pe.wait_ge(oh_ready, i * NG + (j + 1))
                if not (isinstance(i, int) and i * NG + j < before(j)):
                    pe.wait_ge(h_ready, i * NG + (j + 1 - before(j)))
                for c in range(k):
                    mm = nc.tensor.matmul(pre[j % RING][:, c * D:(c + 1) * D], lhsT=lhs[:, j, c * P:(c + 1) * P],
                                          rhs=win[:, j, :], start=True, stop=True)
                mm.then_inc(pre_done, 1)

            def agg_products(i, j, k, bank):
                pe.wait_ge(h_ready, i * NG + (j + 1))
                back = 1 if j == 0 else 2
                if not (isinstance(i, int) and i * NG + j < back):
                    pe.wait_ge(added, i * NG + (j + 1 - back))
                for c in range(k):
                    nc.tensor.matmul(pagg[bank][:, 0:WIN], lhsT=h[:, j % RING, c, :], rhs=onehot[:, j, c, :],
                                     start=(c == 0), stop=(c == k - 1))
                for c in range(k):
                    mm = nc.tensor.matmul(pagg[bank][:, WIN:2 * WIN], lhsT=ones[:, :], rhs=onehot[:, j, c, :],
                                          start=(c == 0), stop=(c == k - 1))
                mm.then_inc(agg_done, 1)

            def body(i):
                gs = groups_of(i)
                for j, off, k in gs:
                    pre_products(i, j, k)
                    if j == 0:
                        if not first(i):
                            agg_products(i - 1, NG - 1, GROUPS[NG - 1], (NG - 1) % 2)
                    else:
                        agg_products(i, j - 1, gs[j - 1][2], (j - 1) % 2)
                    if j == 0 and not (isinstance(i, int) and i < 2):
                        node_products(i - 2)

            with pe.If(bad_v == 0):
                run_iterations(pe, body)
                agg_products(ITERS, len(LAST) - 1, LAST[-1][1], (len(LAST) - 1) % 2)
                for b in range(ITERS - 1, NB):
                    node_products(b)
            with pe.Else():
                def sum_tile(t):
                    pe.wait_ge(g_ef, t * 16 + 16)
                    if not isinstance(t, int):
                        pe.wait_ge(g_sum, t)
                    nc.tensor.matmul(pre[0][:, 0:D], lhsT=sef[:, :], rhs=win[0:DE, 0, :],
                                     start=True, stop=True).then_inc(g_pre, 1)
                    pe.wait_ge(g_h, t + 1)
                    take_waits(pe)
                    with pe.Fori(0, NB) as b:
                        pe.wait_ge(g_oh, t * NB + b + 1)
                        nc.tensor.matmul(pagg[0][:, 0:P], lhsT=sh[:, :], rhs=soh[:, :], start=True, stop=True)
                        nc.tensor.matmul(pagg[0][:, P:2 * P], lhsT=ones[:, :], rhs=soh[:, :],
                                         start=True, stop=True).then_inc(g_mm, 1)
                sum_tile(0)
                with pe.Fori(1, NT) as t:
                    sum_tile(t)
                loop_blocks(pe, node_products)

        @block.vector
        def _(dve):
            def done(n):
                dve.wait_ge(prep, n)

            nc.vector.memset(ones[:, :], 1.0).then_inc(ones_ready, 1)
            nc.vector.memset(aggcnt[:, :, :], 0.0).then_inc(prep, 1)
            dve.wait_ge(iota_ready, 2)
            nc.vector.tensor_copy(iota_f[:, :], iota_i[:, :]).then_inc(prep, 1)
            nc.vector.tensor_copy(node_f[:, :], node_i[:, :]).then_inc(prep, 1)
            dve.wait_ge(tab_in, 48)
            nc.vector.tensor_copy(base_f[:, :], base_i[:, :]).then_inc(prep, 1)
            nc.vector.tensor_copy(dst_f[:, :], dst_i[:, :]).then_inc(prep, 1)
            done(5)
            nc.vector.tensor_scalar(base_col[:, :], base_f[:, :], node_f[:, 0:1], None, ALU.add).then_inc(prep, 1)
            nc.vector.tensor_tensor(slack[:, :], base_f[:, :], open_i[:, :], ALU.subtract).then_inc(prep, 1)
            whole = ITERS * TILES
            d3 = dst_f[:, 0:whole].rearrange("p (i t) -> p i t", t=TILES)
            r3 = rel[:, 0:whole].rearrange("p (i t) -> p i t", t=TILES)
            b3 = base_f[:, 0:ITERS * BPI].rearrange("p (i g) -> p i g", g=BPI)
            for j in range(NG):
                o, k = OFFS[j], GROUPS[j]
                nc.vector.tensor_tensor(r3[:, :, o:o + k], d3[:, :, o:o + k],
                                        b3[:, :, j:j + 1].to_broadcast([P, ITERS, k]), ALU.subtract).then_inc(prep, 1)
            for j, (o, k) in enumerate(LAST):
                nc.vector.tensor_scalar(rel[:, whole + o:whole + o + k], dst_f[:, whole + o:whole + o + k],
                                        base_f[:, ITERS * BPI + j:ITERS * BPI + j + 1], None,
                                        ALU.subtract).then_inc(prep, 1)
            n = 7 + NG + len(LAST)
            done(n)
            nc.vector.tensor_reduce(red[:, 0:1], rel[:, :], AX.X, ALU.max).then_inc(prep, 1)
            nc.vector.tensor_reduce(red[:, 1:2], rel[:, :], AX.X, ALU.min).then_inc(prep, 1)
            nc.vector.tensor_reduce(red[:, 2:3], slack[:, :], AX.X, ALU.min).then_inc(prep, 1)
            done(n + 3)
            nc.vector.tensor_scalar(bad[:, 0:1], red[:, 0:1], float(WIN), None, ALU.is_ge).then_inc(prep, 1)
            nc.vector.tensor_scalar(bad[:, 1:3], red[:, 1:3], 0.0, None, ALU.is_lt).then_inc(prep, 1)
            done(n + 5)
            nc.vector.tensor_reduce(bad[:, 3:4], bad[:, 0:3], AX.X, ALU.add).then_inc(bad_ready, 1)
            dve.wait_ge(bc_in, 48)
            for c in range(NCH):
                lo, hi = c * XCH, min((c + 1) * XCH, NB)
                dve.wait_ge(tab_mm, NCH + c + 1)
                bk = banks[(NCH + c) % len(banks)][:, 0:(hi - lo) * D].rearrange("p (b f) -> p b f", f=D)
                b1v = b1_bc[:, :].rearrange("p (a f) -> p a f", a=1).to_broadcast([P, hi - lo, D])
                nc.vector.tensor_tensor(pst[:, 1, lo:hi, :], bk, b1v, ALU.add).then_inc(pdst_sb, 1)
            dve.wait_ge(bad_mm, 1)
            nc.vector.tensor_copy(flag[:, :], pmisc[0:1, 0:1]).then_inc(flag_ready, 1)
            dve.wait_ge(x_in, 16)
            dve.wait_ge(flag_ready, 1)
            bad_v = dve.value_load(flag[0:1, 0:1], min_val=0, max_val=3 * P)

            def first(b):
                return isinstance(b, int) and b == 0

            NEWTON = 3
            RS = 4 + 2 * NEWTON
            CHAIN = 12 + 2 * RS

            def aggr_after(count):
                dve.wait_ge(chain, count)
                if not isinstance(count, int):
                    take_waits(dve)

            def gate_sum(b):
                dve.wait_ge(node_mm, b + 1)
                nc.vector.tensor_scalar(rcp[:, 0:1], pna[:, 2 * D:2 * D + 1], 1.0, None, ALU.max).then_inc(chain, 1)
                dve.wait_ge(chain, b * CHAIN + 1)
                nc.vector.reciprocal(rcp[:, 1:2], rcp[:, 0:1]).then_inc(chain, 1)
                dve.wait_ge(chain, b * CHAIN + 2)
                dve.wait_ge(xg_ready, b + 1)
                if not first(b):
                    dve.wait_ge(th_ready, b)
                nc.vector.scalar_tensor_tensor(out=gt[:, :], in0=pna[:, 0:2 * D], scalar=rcp[:, 1:2], in1=xg[:, :],
                                               op0=ALU.mult, op1=ALU.add).then_inc(gt_ready, 1)

            def rsqrt(b, n):
                nc.vector.tensor_scalar(nt[:, 0:1], mv[:, 1:2], EPS, None, ALU.add).then_inc(chain, 1)
                dve.wait_ge(chain, b * CHAIN + (n + 1))
                nc.vector.tensor_scalar(nhv[:, :], nt[:, 0:1], -0.5, None, ALU.mult).then_inc(chain, 1)
                nc.vector.tensor_scalar(yi[:, 0:1], nt[:, 0:1].bitcast(I32), 1, None,
                                        ALU.logical_shift_right).then_inc(chain, 1)
                dve.wait_ge(chain, b * CHAIN + (n + 3))
                nc.vector.tensor_scalar(yi[:, 1:2], yi[:, 0:1], -1.0, float(0x5F3759DF), ALU.mult,
                                        ALU.add).then_inc(chain, 1)
                dve.wait_ge(chain, b * CHAIN + (n + 4))
                y = yi[:, 1:2].bitcast(F32)
                for s in range(NEWTON):
                    nc.vector.scalar_tensor_tensor(out=nt[:, 1:2], in0=y, scalar=y, in1=nhv[:, :],
                                                   op0=ALU.mult, op1=ALU.mult).then_inc(chain, 1)
                    dve.wait_ge(chain, b * CHAIN + (n + 5 + 2 * s))
                    z = nt[:, 3:4] if s % 2 == 0 else nt[:, 2:3]
                    nc.vector.scalar_tensor_tensor(out=z, in0=nt[:, 1:2], scalar=1.5, in1=y,
                                                   op0=ALU.add, op1=ALU.mult).then_inc(chain, 1)
                    dve.wait_ge(chain, b * CHAIN + (n + 6 + 2 * s))
                    y = z
                return y

            def mix_in(b):
                dve.wait_ge(th_ready, b + 1)
                xv = x_all[:, bass.ds(b, 1), :].rearrange("p a f -> p (a f)")
                nc.vector.tensor_tensor(diff[:, :], xv, th[:, D:2 * D], ALU.subtract).then_inc(chain, 1)
                nc.vector.tensor_tensor(xb[:, :], xv, beta_bc[:, :], ALU.add).then_inc(chain, 1)
                dve.wait_ge(chain, b * CHAIN + 4)
                nc.vector.scalar_tensor_tensor(out=mix[:, :], in0=th[:, 0:D], scalar=1.0, in1=diff[:, :],
                                               op0=ALU.add, op1=ALU.mult).then_inc(chain, 1)
                dve.wait_ge(chain, b * CHAIN + 5)
                nc.vector.scalar_tensor_tensor(out=upd[:, :], in0=mix[:, :], scalar=0.5, in1=th[:, D:2 * D],
                                               op0=ALU.mult, op1=ALU.add).then_inc(upd_ready, 1)
                dve.wait_ge(upd_ready, b + 1)
                nc.vector.bn_stats(stats[:, :], upd[:, :]).then_inc(chain, 1)
                aggr_after(b * CHAIN + 6)
                nc.vector.bn_aggr(mv[:, :], stats[:, :]).then_inc(chain, 1)
                dve.wait_ge(chain, b * CHAIN + 7)

            def norm_in(b):
                r = rsqrt(b, 7)
                n = 7 + RS
                nc.vector.tensor_scalar(nrm[:, :], upd[:, :], mv[:, 0:1], r, ALU.subtract, ALU.mult).then_inc(chain, 1)
                dve.wait_ge(chain, b * CHAIN + (n + 1))
                nc.vector.tensor_tensor(ynew[:, :], nrm[:, :], gamma_bc[:, :], ALU.mult).then_inc(chain, 1)
                dve.wait_ge(chain, b * CHAIN + (n + 2))
                nc.vector.tensor_tensor(ysum[:, :], ynew[:, :], xb[:, :], ALU.add).then_inc(chain, 1)
                dve.wait_ge(chain, b * CHAIN + (n + 3))

            def norm_out(b):
                n = 10 + RS
                nc.vector.bn_stats(stats[:, :], ysum[:, :]).then_inc(chain, 1)
                aggr_after(b * CHAIN + (n + 1))
                nc.vector.bn_aggr(mv[:, :], stats[:, :]).then_inc(chain, 1)
                dve.wait_ge(chain, b * CHAIN + (n + 2))
                r = rsqrt(b, n + 2)
                if not first(b):
                    dve.wait_ge(out_done, b * 16)
                nc.vector.tensor_scalar(oblk[:, :], ysum[:, :], mv[:, 0:1], r, ALU.subtract,
                                        ALU.mult).then_inc(out_ready, 1)


            def prepare(i, j, off, k):
                dve.wait_ge(slot_in[j], i * 48 + 48)
                nc.vector.tensor_scalar(lhs[DE:P, j, 0:k * P], dstb[DE:P, j, 0:k * P],
                                        base_col[DE:P, bass.ds(i * BPI + j, 1)], None, ALU.is_equal).then_inc(ohT_done, 1)
                if not (isinstance(i, int) and i == 0):
                    dve.wait_ge(agg_done, i * NG + (j + 1 - NG))
                i0 = iota_f[:, 0:WIN].rearrange("p (a w) -> p a w", a=1).to_broadcast([P, k, WIN])
                r0 = rel[:, bass.ds(i * TILES + off, k)].rearrange("p (k a) -> p k a", a=1).to_broadcast([P, k, WIN])
                nc.vector.tensor_tensor(onehot[:, j, 0:k, :], i0, r0, ALU.is_equal).then_inc(oh_ready, 1)

            def add_rows(i, j, k):
                dve.wait_ge(pre_done, i * NG + (j + 1))
                dve.wait_ge(gath_in[j], i * (16 * k) + 16 * k if not (isinstance(i, int) and i == ITERS)
                            else ITERS * 16 * GROUPS[j] + 16 * k)
                z = pre[j % RING][:, 0:k * D].rearrange("p (c f) -> p c f", f=D)
                nc.vector.tensor_tensor(z, z, gath[:, j, 0:k, :], ALU.add).then_inc(sum_done, 1)

            def add_window(i, j, bank):
                base = load_base(dve, i, j)
                dve.wait_ge(agg_done, i * NG + (j + 1))
                if not (isinstance(i, int) and i * NG + j == 0):
                    dve.wait_ge(added, i * NG + j)
                w = aggcnt[:, :, bass.ds(base, WIN)]
                nc.vector.tensor_tensor(w, w, pagg[bank][:, 0:2 * WIN].rearrange("p (a w) -> p a w", a=2),
                                        ALU.add).then_inc(added, 1)

            def body(i, last=False):
                gs = groups_of(i)
                final = isinstance(i, int) and i == ITERS
                for j, off, k in gs:
                    if j + 1 < len(gs):
                        prepare(i, j + 1, gs[j + 1][1], gs[j + 1][2])
                    elif last:
                        prepare(ITERS, 0, *LAST[0])
                    elif not final:
                        prepare(i + 1, 0, OFFS[0], GROUPS[0])
                    add_rows(i, j, k)
                    if j == 0:
                        if not first(i):
                            add_window(i - 1, NG - 1, (NG - 1) % 2)
                    else:
                        add_window(i, j - 1, (j - 1) % 2)
                    if not (isinstance(i, int) and i < 2) and not final:
                        if j == 1:
                            gate_sum(i - 2)
                        if j == 2:
                            mix_in(i - 2)
                        if j == 3:
                            norm_in(i - 2)
                        if j == 4:
                            norm_out(i - 2)

            with dve.If(bad_v == 0):
                prepare(0, 0, OFFS[0], GROUPS[0])
                for i in range(3):
                    body(i)
                with dve.Fori(3, ITERS - 1) as i:
                    body(i)
                body(ITERS - 1, last=True)
                body(ITERS)
                add_window(ITERS, len(LAST) - 1, (len(LAST) - 1) % 2)
                for b in range(ITERS - 2, NB):
                    gate_sum(b)
                    mix_in(b)
                    norm_in(b)
                    norm_out(b)
            with dve.Else():
                def sum_tile(t):
                    dve.wait_ge(g_pre, t + 1)
                    dve.wait_ge(g_gath, t * 32 + 32)
                    if not isinstance(t, int):
                        dve.wait_ge(g_h, t)
                    nc.vector.tensor_tensor(pre[1][:, 0:D], pre[0][:, 0:D], sgath[:, 0, :], ALU.add).then_inc(g_sum0, 1)
                    dve.wait_ge(g_sum0, t + 1)
                    nc.vector.tensor_tensor(pre[1][:, 0:D], pre[1][:, 0:D], sgath[:, 1, :], ALU.add).then_inc(g_sum, 1)
                    if not isinstance(t, int):
                        dve.wait_ge(g_oh, t * NB)
                    nc.vector.tensor_copy(shift[:, :], dst_f[:, bass.ds(t, 1)]).then_inc(g_shift, 1)
                    with dve.Fori(0, NB) as b:
                        dve.wait_ge(g_shift, t * (NB + 1) + b + 1)
                        nc.vector.tensor_scalar(soh[:, :], iota_f[:, :], shift[:, 0:1], None,
                                                ALU.is_equal).then_inc(g_oh, 1)
                        dve.wait_ge(g_oh, t * NB + b + 1)
                        nc.vector.tensor_scalar(shift[:, :], shift[:, :], float(P), None,
                                                ALU.subtract).then_inc(g_shift, 1)
                        dve.wait_ge(g_mm, t * NB + b + 1)
                        w = aggcnt[:, :, bass.ds(b * P, P)]
                        nc.vector.tensor_tensor(w, w, pagg[0][:, 0:2 * P].rearrange("p (a w) -> p a w", a=2),
                                                ALU.add).then_inc(g_added, 1)
                    dve.wait_ge(g_added, t * NB + NB)
                sum_tile(0)
                with dve.Fori(1, NT) as t:
                    sum_tile(t)

                def stage(b):
                    gate_sum(b)
                    mix_in(b)
                    norm_in(b)
                    norm_out(b)
                loop_blocks(dve, stage)


def kernel(x, src, dst, edge_attr_64, L0_gnn_W1, L0_gnn_b1, L0_gnn_W2, L0_gnn_b2, L0_gnn_Wg, L0_gnn_bg,
           L0_gnn_Wt, L0_gnn_bt, L0_gnn_gamma, L0_gnn_beta):
    import concourse.bacc as _bacc
    from concourse.bass_utils import run_bass_kernel_spmd as _run

    x, src, dst, ef = (np.asarray(a) for a in (x, src, dst, edge_attr_64))
    n, e = x.shape[0], src.shape[0]
    nb, nt, iters, last = shapes(n, e)
    src_p = np.concatenate([src, np.zeros(nt * P - e, src.dtype)])
    dst_p = np.concatenate([dst, np.full(nt * P - e, n, dst.dtype)])
    x_p = np.concatenate([x, np.zeros((nb * P - n, D), x.dtype)])
    ef_p = np.concatenate([ef, np.zeros((nt * P - e, DE), ef.dtype)])
    starts, opened = np.zeros((iters + 1, BPI), np.int64), np.zeros((iters + 1, BPI), np.int32)
    for i in range(iters + 1):
        offs = OFFS if i < iters else [o for o, _ in last]
        for j in range(BPI):
            jj = min(j, len(offs) - 1)
            starts[i, j] = (i * TILES + offs[jj]) * P
            opened[i, j] = P * max(i if jj >= AHEAD else i - 1, 0)
    arrays = {
        "x": x_p, "xT": x_p.T, "src_pt": src_p.reshape(nt, P).T, "dst_pt": dst_p.reshape(nt, P).T,
        "dst_flat": dst_p.reshape(1, -1), "base_tab": dst_p[starts.ravel()].reshape(1, -1),
        "open_tab": opened.reshape(1, -1), "efT": ef_p.T,
        "W1": L0_gnn_W1, "b1": np.asarray(L0_gnn_b1).reshape(1, -1), "W2T": np.asarray(L0_gnn_W2).T,
        "b2": np.asarray(L0_gnn_b2).reshape(-1, 1), "Wg": L0_gnn_Wg, "bg": np.asarray(L0_gnn_bg).reshape(1, -1),
        "Wt": L0_gnn_Wt, "bt": np.asarray(L0_gnn_bt).reshape(1, -1),
        "gamma": np.asarray(L0_gnn_gamma).reshape(1, -1), "beta": np.asarray(L0_gnn_beta).reshape(1, -1),
    }
    arrays = {f"in_{k}": np.ascontiguousarray(v) for k, v in arrays.items()}
    nc = _bacc.Bacc("TRN2", target_bir_lowering=False, num_devices=1)
    args = [nc.dram_tensor(k, v.shape, mybir.dt.from_np(v.dtype), kind="ExternalInput").ap() for k, v in arrays.items()]
    out = nc.dram_tensor("out_x", (n, D), F32, kind="ExternalOutput").ap()
    gnn_kernel(nc, *args, out)
    r = _run(nc, [arrays], core_ids=[0])
    return r.results[0]["out_x"]
```

```python
import math
from contextlib import ExitStack

import numpy as np
import concourse.bass as bass
from concourse import mybir

ALU = mybir.AluOpType
ACT = mybir.ActivationFunctionType
AX = mybir.AxisListType
F32 = mybir.dt.float32
I32 = mybir.dt.int32

P = 128
D = 128
DE = 64
WIN = 64
EPS = 1e-5

GROUPS = (4, 4, 3, 3, 3)
OFFS = (0, 4, 8, 11, 14)
NG = len(GROUPS)
TILES = sum(GROUPS)
KMAX = max(GROUPS)
BPI = 8
VR = 33
LOOK = 2
AHEAD = 3


def shapes(n_nodes, n_edges):
    blocks = -(-n_nodes // P)
    tiles = -(-n_edges // P)
    iters = min(tiles // TILES, blocks - 1)
    last = []
    left = tiles - iters * TILES
    off = 0
    while left > 0:
        k = min(KMAX, left)
        last.append((off, k))
        off += k
        left -= k
    assert last == list(zip(OFFS, GROUPS))[:len(last)] and len(last) == LOOK and iters >= 4
    return blocks, tiles, iters, last


def gnn_kernel(nc, x, xT, src_pt, dst_pt, dst_flat, base_tab, open_tab, efT,
               W1, b1, W2T, b2, Wg, bg, Wt, bt, gamma, beta, out):
    N = out.shape[0]
    NP = x.shape[0]
    NB, NT, ITERS, LAST = shapes(N, dst_pt.shape[1] * P)
    assert NP == NB * P and D == P
    NBASE = base_tab.shape[1]
    ROWS_LAST = N - (NB - 1) * P
    RING = 3

    NS = 3

    def before(j):
        for back in range(1, NG + 1):
            if (j - back) % NG % RING == j % RING:
                return back

    with ExitStack() as ctx:
        def sb(name, shape, dt=F32):
            return ctx.enter_context(nc.sbuf_tensor(name, shape, dt))

        def ps(name, shape):
            return ctx.enter_context(nc.psum_tensor(name, shape, F32))

        def sem(name):
            return ctx.enter_context(nc.semaphore(name))

        psrc_d = nc.dram_tensor("psrc_d", [NP, D], F32).ap()
        pdst_d = nc.dram_tensor("pdst_d", [NP, D], F32).ap()

        xT_all = sb("xT_all", [P, NP])
        x_all = sb("x_all", [P, NB, D])
        w1s = sb("w1s", [P, D])
        w1d = sb("w1d", [P, D])
        w2T = sb("w2T", [P, D])
        wx = sb("wx", [P, 2 * D])
        wa = sb("wa", [P, 2 * D])
        w2a = sb("w2a", [P, 2 * D])
        b2c = sb("b2c", [P, 1])
        vec = sb("vec", [VR, 2 * D])
        b1_bc = sb("b1_bc", [P, D])
        gamma_bc = sb("gamma_bc", [P, D])
        beta_bc = sb("beta_bc", [P, D])
        ones = sb("ones", [P, P])
        iota_i = sb("iota_i", [P, P], I32)
        iota_f = sb("iota_f", [P, P])
        node_i = sb("node_i", [P, 1], I32)
        node_f = sb("node_f", [P, 1])
        src_i = sb("src_i", [P, src_pt.shape[1]], I32)
        dst_i = sb("dst_i", [P, NT], I32)
        base_i = sb("base_i", [P, NBASE], I32)
        open_i = sb("open_i", [P, NBASE], I32)
        base_f = sb("base_f", [P, NBASE])
        base_col = sb("base_col", [P, NBASE])
        slack = sb("slack", [P, NBASE])
        rel = sb("rel", [P, NT])
        dst_f = sb("dst_f", [P, NT])
        red = sb("red", [P, 4])
        bad = sb("bad", [P, 4])
        flag = sb("flag", [1, 1], I32)
        aggcnt = sb("aggcnt", [P, 1 + KMAX, NP])
        pst = sb("pst", [P, 2, NB, D])

        idx = sb("idx", [P, NG, KMAX], I32)
        lhs = sb("lhs", [P, NG, KMAX * P])
        dstb = sb("dstb", [P, NG, KMAX * P], I32)
        win = sb("win", [P, NG, D])
        gath = sb("gath", [P, NG, KMAX, D])
        onehot = sb("onehot", [P, NG, KMAX, WIN])
        h = sb("h", [P, RING, KMAX, D])

        xT_blk = [sb(f"xT_blk{s}", [P, P]) for s in range(NS)]
        ablk = [sb(f"ablk{s}", [P, P]) for s in range(NS)]
        cblk = [sb(f"cblk{s}", [VR, P]) for s in range(NS)]
        xg = [sb(f"xg{s}", [P, 2 * D]) for s in range(NS)]
        gt = [sb(f"gt{s}", [P, 2 * D]) for s in range(NS)]
        th = [sb(f"th{s}", [P, 2 * D]) for s in range(NS)]
        rcp = [sb(f"rcp{s}", [P, 1]) for s in range(NS)]
        diff = [sb(f"diff{s}", [P, D]) for s in range(NS)]
        mix = [sb(f"mix{s}", [P, D]) for s in range(NS)]
        upd = [sb(f"upd{s}", [P, D]) for s in range(NS)]
        xb = [sb(f"xb{s}", [P, D]) for s in range(NS)]
        nrm = [sb(f"nrm{s}", [P, D]) for s in range(NS)]
        ysum = [sb(f"ysum{s}", [P, D]) for s in range(NS)]
        ynew = [sb(f"ynew{s}", [P, D]) for s in range(NS)]
        stats = [sb(f"stats{s}", [P, 6]) for s in range(NS)]
        mv = [sb(f"mv{s}", [P, 2]) for s in range(NS)]
        nhv = [sb(f"nhv{s}", [P, 1]) for s in range(NS)]
        yi = [sb(f"yi{s}", [P, 1], I32) for s in range(NS)]
        nt = [sb(f"nt{s}", [P, 4]) for s in range(NS)]
        oblk = [sb(f"oblk{s}", [P, D]) for s in range(NS)]

        sidx = sb("sidx", [P, 2], I32)
        sef = sb("sef", [DE, P])
        sgath = sb("sgath", [P, 2, D])
        sh = sb("sh", [P, D])
        shift = sb("shift", [P, 1])
        soh = sb("soh", [P, P])

        pre = [ps(f"pre{r}", [P, KMAX * D]) for r in range(RING)]
        pagg = [ps(f"pagg{r}", [P, 512]) for r in range(RING)]
        pnx = ps("pnx", [P, 512])
        pna = ps("pna", [P, 512])
        pmisc = pagg[2]
        px = [pnx, pre[0], pre[1]]
        pa = [pna, pre[2], pagg[0]]
        banks = pre + pagg[0:2] + [pnx, pna]

        XCH = 4
        NCH = -(-NB // XCH)
        w1_in = sem("w1_in")
        xT_in = [sem(f"xT_in{c}") for c in range(NCH)]
        tab_in = sem("tab_in")
        wgt_in = sem("wgt_in")
        bc_in = sem("bc_in")
        src_in = sem("src_in")
        win_in = sem("win_in")
        x_in = sem("x_in")
        ones_ready = sem("ones_ready")
        iota_ready = sem("iota_ready")
        tab_mm = sem("tab_mm")
        psrc_sb = sem("psrc_sb")
        pdst_sb = sem("pdst_sb")
        psrc_out = sem("psrc_out")
        pdst_out = sem("pdst_out")
        prep = sem("prep")
        bad_ready = sem("bad_ready")
        bad_mm = sem("bad_mm")
        flag_ready = sem("flag_ready")
        vec_zero = sem("vec_zero")
        half = sem("half")
        fold_mm = sem("fold_mm")
        fold_ready = sem("fold_ready")
        slot_in = [sem(f"slot_in{j}") for j in range(NG)]
        gath_in = [sem(f"gath_in{j}") for j in range(NG)]
        idx_ready = sem("idx_ready")
        away_ready = sem("away_ready")
        ohT_ready = sem("ohT_ready")
        oh_ready = sem("oh_ready")
        pre_done = sem("pre_done")
        sum_done = sem("sum_done")
        h_ready = sem("h_ready")
        agg_done = sem("agg_done")
        added = sem("added")
        passed = sem("passed")
        xT_blk_in = sem("xT_blk_in")
        xT_last_in = sem("xT_last_in")
        ablk_ready = sem("ablk_ready")
        node_mm = sem("node_mm")
        xg_ready = sem("xg_ready")
        gt_ready = sem("gt_ready")
        th_ready = sem("th_ready")
        upd_ready = sem("upd_ready")
        chain = [sem(f"chain{s}") for s in range(NS)]
        cnt_ready = sem("cnt_ready")
        cblk_ready = sem("cblk_ready")
        out_ready = sem("out_ready")
        out_done = sem("out_done")
        g_idx_half = sem("g_idx_half")
        g_idx = sem("g_idx")
        g_ef = sem("g_ef")
        g_gath = sem("g_gath")
        g_pre = sem("g_pre")
        g_sum0 = sem("g_sum0")
        g_sum = sem("g_sum")
        g_h = sem("g_h")
        g_shift = sem("g_shift")
        g_oh = sem("g_oh")
        g_mm = sem("g_mm")
        g_added = sem("g_added")

        block = ctx.enter_context(nc.Block())

        def groups_of(i):
            if isinstance(i, int) and i == ITERS:
                return [(j, off, k) for j, (off, k) in enumerate(LAST)]
            return list(zip(range(NG), OFFS, GROUPS))

        ENDING = [(b, 1 + n, 0) for n, b in enumerate(range(ITERS - 1, NB))]
        assert len(ENDING) < NS

        def in_turn(b):
            return (b, 0, b)

        def fresh(m):
            return isinstance(m, int) and m == 0

        def take_waits(eng):
            eng.sem_inc(passed, 1)

        def near(i, j, d):
            up, jj = divmod(j + d, NG)
            ii = i + up if up else i
            if isinstance(ii, int) and (ii < 0 or ii > ITERS or ii == ITERS and jj >= len(LAST)):
                return None
            return ii, jj, OFFS[jj], GROUPS[jj]

        def run_iterations(eng, body):
            for i in range(3):
                body(i)
            with eng.Fori(3, ITERS) as i:
                body(i)
            body(ITERS)

        def load_base(eng, i, j):
            return eng.value_load(base_i[0:1, bass.ds(i * BPI + j, 1)], min_val=0, max_val=N)

        def loop_blocks(eng, stage):
            stage(0)
            with eng.Fori(1, NB - 1) as b:
                stage(b)
            stage(NB - 1)

        @block.sync
        def _(sp):
            sp.dma_start(w1s[:, :], W1[0:D, :]).then_inc(w1_in, 16)
            sp.dma_start(w1d[:, :], W1[D:2 * D, :]).then_inc(w1_in, 16)
            for c in range(NCH):
                lo, hi = c * XCH * P, min((c + 1) * XCH, NB) * P
                sp.dma_start(xT_all[:, lo:hi], xT[:, lo:hi]).then_inc(xT_in[c], 16)
            sp.dma_start(win[0:DE, :, :], W1[2 * D:2 * D + DE, :].rearrange("k (a n) -> k a n", a=1)
                         .to_broadcast([DE, NG, D])).then_inc(win_in, 16)
            sp.dma_start(x_all[:, :, :], x.rearrange("(b p) f -> p b f", p=P)).then_inc(x_in, 16)
            for t, (d, ready, sent) in enumerate(((psrc_d, psrc_sb, psrc_out), (pdst_d, pdst_sb, pdst_out))):
                dv = d.rearrange("(b p) f -> p b f", p=P)
                for c in range(NCH):
                    lo, hi = c * XCH, min((c + 1) * XCH, NB)
                    sp.wait_ge(ready, c + 1)
                    sp.dma_start(dv[:, lo:hi, :], pst[:, t, lo:hi, :]).then_inc(sent, 16)
            sp.wait_ge(pdst_out, 16 * NCH)
            sp.wait_ge(win_in, 16)
            sp.wait_ge(flag_ready, 1)
            bad_v = sp.value_load(flag[0:1, 0:1], min_val=0, max_val=3 * P)

            def xT_load(b):
                if not (isinstance(b, int) and b == 0):
                    sp.wait_ge(node_mm, b)
                sp.dma_start(xT_blk[0][:, :], xT[:, bass.ds(b * P, P)]).then_inc(xT_blk_in, 16)

            def out_store(b, s=0):
                sp.wait_ge(out_ready, b + 1)
                if isinstance(b, int) and b == NB - 1:
                    sp.dma_start(out[b * P:N, :], oblk[s][0:ROWS_LAST, :]).then_inc(out_done, 16)
                else:
                    sp.dma_start(out[bass.ds(b * P, P), :], oblk[s][:, :]).then_inc(out_done, 16)

            def body(i):
                for j, off, k in groups_of(i):
                    if not (isinstance(i, int) and i == 0):
                        sp.wait_ge(pre_done, i * NG + (j - NG + 1))
                    e0 = (i * TILES + off) * P
                    base = load_base(sp, i, j)
                    sp.dma_start(dstb[DE:P, j, 0:k * P],
                                 dst_flat[0:1, bass.ds(e0, k * P)].to_broadcast([WIN, k * P])).then_inc(slot_in[j], 16)
                    sp.dma_start(lhs[0:DE, j, 0:k * P], efT[:, bass.ds(e0, k * P)]).then_inc(slot_in[j], 16)
                    sp.dma_start(win[DE:P, j, :], pdst_d[bass.ds(base, WIN), :]).then_inc(slot_in[j], 16)
                    if j == 1 and not (isinstance(i, int) and i < 2):
                        xT_load(i - 2)
                if not (isinstance(i, int) and (i < 3 or i == ITERS)):
                    out_store(i - 3)

            with sp.If(bad_v == 0):
                run_iterations(sp, body)
                for b, s, _ in ENDING:
                    sp.dma_start(xT_blk[s][:, :], xT[:, b * P:(b + 1) * P]).then_inc(xT_last_in, 16)
                out_store(ITERS - 3)
                out_store(ITERS - 2)
                for b, s, _ in ENDING:
                    out_store(b, s)
            with sp.Else():
                def load_tile(t):
                    if not isinstance(t, int):
                        sp.wait_ge(g_pre, t)
                    sp.dma_start(sef[:, :], efT[:, bass.ds(t * P, P)]).then_inc(g_ef, 16)
                load_tile(0)
                with sp.Fori(1, NT) as t:
                    load_tile(t)

                def stage(b):
                    xT_load(b)
                    out_store(b)
                loop_blocks(sp, stage)
            sp.wait_ge(out_done, 16 * NB)

        @block.gpsimd
        def _(pool):
            nc.gpsimd.iota(iota_i[:, :], pattern=[[1, P]], base=0, channel_multiplier=0).then_inc(iota_ready, 1)
            nc.gpsimd.iota(node_i[:, :], pattern=[[0, 1]], base=WIN, channel_multiplier=-1).then_inc(iota_ready, 1)
            pool.wait_ge(flag_ready, 1)
            bad_v = pool.value_load(flag[0:1, 0:1], min_val=0, max_val=3 * P)

            def body(i):
                for j, off, k in groups_of(i):
                    pool.wait_ge(idx_ready, i * NG + (j + 1))
                    if not (isinstance(i, int) and i == 0):
                        pool.wait_ge(sum_done, i * NG + (j - NG + 1))
                        take_waits(pool)
                    for c in range(k):
                        nc.gpsimd.indirect_dma_start(
                            out=gath[:, j, c, :], out_offset=None, in_=psrc_d,
                            in_offset=bass.IndirectOffsetOnAxis(ap=idx[:, j, c:c + 1], axis=0)).then_inc(gath_in[j], 16)

            pool.wait_ge(psrc_out, 16 * NCH)
            with pool.If(bad_v == 0):
                run_iterations(pool, body)
            with pool.Else():
                pool.wait_ge(pdst_out, 16 * NCH)

                def gather_tile(t):
                    pool.wait_ge(g_idx, t + 1)
                    if not isinstance(t, int):
                        pool.wait_ge(g_sum, t)
                        take_waits(pool)
                    for c, table in enumerate((psrc_d, pdst_d)):
                        nc.gpsimd.indirect_dma_start(
                            out=sgath[:, c, :], out_offset=None, in_=table,
                            in_offset=bass.IndirectOffsetOnAxis(ap=sidx[:, c:c + 1], axis=0)).then_inc(g_gath, 16)
                gather_tile(0)
                with pool.Fori(1, NT) as t:
                    gather_tile(t)

        @block.scalar
        def _(act):
            act.dma_start(src_i[:, :], src_pt).then_inc(src_in, 16)
            act.dma_start(dst_i[:, :], dst_pt).then_inc(tab_in, 16)
            act.dma_start(base_i[:, :], base_tab.to_broadcast([P, NBASE])).then_inc(tab_in, 16)
            act.dma_start(open_i[:, :], open_tab.to_broadcast([P, NBASE])).then_inc(tab_in, 16)
            act.dma_start(b1_bc[:, :], b1.to_broadcast([P, D])).then_inc(bc_in, 16)
            act.dma_start(gamma_bc[:, :], gamma.to_broadcast([P, D])).then_inc(bc_in, 16)
            act.dma_start(beta_bc[:, :], beta.to_broadcast([P, D])).then_inc(bc_in, 16)
            act.wait_ge(vec_zero, 1)
            for dst_ap, src_ap in ((wx[:, 0:D], Wg[0:D, :]), (wx[:, D:2 * D], Wt[0:D, :]),
                                   (wa[:, 0:D], Wg[D:2 * D, :]), (wa[:, D:2 * D], Wt[D:2 * D, :]),
                                   (vec[VR - 1:VR, 0:D], bg), (vec[VR - 1:VR, D:2 * D], bt),
                                   (w2T[:, :], W2T), (b2c[:, :], b2)):
                act.dma_start(dst_ap, src_ap).then_inc(wgt_in, 16)
            act.wait_ge(ones_ready, 1)
            nc.scalar.activation(sh[:, 0:1], ones[:, 0:1], ACT.Silu).then_inc(half, 1)
            for c in range(0, NCH):
                lo, hi = c * XCH, min((c + 1) * XCH, NB)
                act.wait_ge(tab_mm, c + 1)
                nc.scalar.activation(pst[:, 0, lo:hi, :], banks[c % len(banks)][:, 0:(hi - lo) * D]
                                     .rearrange("p (b f) -> p b f", f=D), ACT.Copy).then_inc(psrc_sb, 1)
            act.wait_ge(wgt_in, 16 * 8)
            for w in (wx[:, 0:D], wa[:, 0:D], vec[VR - 1:VR, 0:D]):
                nc.scalar.activation(w, w, ACT.Copy, scale=0.5).then_inc(half, 1)
            act.wait_ge(src_in, 16)
            for j in range(NG):
                nc.scalar.activation(idx[:, j, 0:GROUPS[j]], src_i[:, OFFS[j]:OFFS[j] + GROUPS[j]],
                                     ACT.Copy).then_inc(idx_ready, 1)
            act.wait_ge(fold_mm, 1)
            nc.scalar.activation(w2a[:, :], pmisc[:, 0:2 * D], ACT.Copy).then_inc(fold_ready, 1)
            nc.scalar.activation(vec[0:1, :], pmisc[0:1, 2 * D:4 * D], ACT.Copy).then_inc(fold_ready, 1)

            act.wait_ge(flag_ready, 1)
            bad_v = act.value_load(flag[0:1, 0:1], min_val=0, max_val=3 * P)

            def first(b):
                return isinstance(b, int) and b == 0

            def stage_copy(b, s, m):
                if not fresh(m):
                    act.wait_ge(node_mm, b)
                nc.scalar.activation(ablk[s][:, :], aggcnt[:, 0, bass.ds(b * P, P)], ACT.Copy).then_inc(ablk_ready, 1)

            def stage_xg(b, s, m):
                act.wait_ge(node_mm, b + 1)
                if not fresh(m):
                    act.wait_ge(gt_ready, b)
                nc.scalar.activation(xg[s][:, :], px[s][:, 0:2 * D], ACT.Copy).then_inc(xg_ready, 1)

            def stage_tanh(b, s, m):
                act.wait_ge(gt_ready, b + 1)
                if not fresh(m):
                    act.wait_ge(upd_ready, b)
                nc.scalar.activation(th[s][:, :], gt[s][:, :], ACT.Tanh).then_inc(th_ready, 1)

            def onehot_T(i, j, off, k):
                act.wait_ge(slot_in[j], i * 48 + 48)
                nc.scalar.activation(lhs[DE:P, j, 0:k * P], dstb[DE:P, j, 0:k * P], ACT.Abs,
                                     bias=base_col[DE:P, bass.ds(i * BPI + j, 1)]).then_inc(away_ready, 1)
                act.wait_ge(away_ready, i * NG + (j + 1))
                nc.scalar.activation(lhs[DE:P, j, 0:k * P], lhs[DE:P, j, 0:k * P], ACT.Relu, bias=1.0,
                                     scale=-1.0).then_inc(ohT_ready, 1)

            def silu(i, j, off, k):
                act.wait_ge(sum_done, i * NG + (j + 1))
                if not (isinstance(i, int) and i * NG + j < before(j)):
                    act.wait_ge(agg_done, i * NG + (j + 1 - before(j)))
                nc.scalar.activation(h[:, j % RING, 0:k, :], pre[j % RING][:, 0:k * D]
                                     .rearrange("p (c f) -> p c f", f=D), ACT.Silu).then_inc(h_ready, 1)

            def next_idx(i, j, off, k):
                nc.scalar.activation(idx[:, j, 0:k], src_i[:, bass.ds(i * TILES + (TILES + off), k)],
                                     ACT.Copy).then_inc(idx_ready, 1)

            def body(i):
                final = isinstance(i, int) and i == ITERS
                for j, off, k in groups_of(i):
                    if near(i, j, 2):
                        onehot_T(*near(i, j, 2))
                    silu(i, j, off, k)
                    if not final:
                        next_idx(i, j, off, k)
                    if j == NG - 1 and not first(i):
                        act.wait_ge(added, i * NG + AHEAD)
                        stage_copy(*in_turn(i - 1))
                    if not (isinstance(i, int) and i < 2):
                        if j == 1:
                            stage_xg(*in_turn(i - 2))
                            stage_tanh(*in_turn(i - 2))

            with act.If(bad_v == 0):
                onehot_T(*near(0, 0, 0))
                onehot_T(*near(0, 0, 1))
                run_iterations(act, body)
                act.wait_ge(added, ITERS * NG + len(LAST))
                for e in ENDING:
                    stage_copy(*e)
                for e in ENDING:
                    stage_xg(*e)
                for e in ENDING:
                    stage_tanh(*e)
            with act.Else():
                def idx_tile(t):
                    if not isinstance(t, int):
                        act.wait_ge(g_gath, 32 * t)
                    nc.scalar.activation(sidx[:, 0:1], src_i[:, bass.ds(t, 1)], ACT.Copy).then_inc(g_idx_half, 1)
                    nc.scalar.activation(sidx[:, 1:2], dst_i[:, bass.ds(t, 1)], ACT.Copy).then_inc(g_idx, 1)
                    act.wait_ge(g_sum, t + 1)
                    if not isinstance(t, int):
                        act.wait_ge(g_mm, t * NB)
                    nc.scalar.activation(sh[:, :], pre[1][:, 0:D], ACT.Silu).then_inc(g_h, 1)
                idx_tile(0)
                with act.Fori(1, NT) as t:
                    idx_tile(t)
                act.wait_ge(g_added, NT * NB)

                def stage(b):
                    stage_copy(*in_turn(b))
                    stage_xg(*in_turn(b))
                    stage_tanh(*in_turn(b))
                loop_blocks(act, stage)

        @block.tensor
        def _(pe):
            pe.wait_ge(w1_in, 32)
            n = 0
            for w in (w1s, w1d):
                for c in range(NCH):
                    lo, hi = c * XCH, min((c + 1) * XCH, NB)
                    if w is w1s:
                        pe.wait_ge(xT_in[c], 16)
                    if n >= len(banks):
                        m = n - len(banks)
                        pe.wait_ge(*((psrc_sb, m + 1) if m < NCH else (pdst_sb, m - NCH + 1)))
                    for b in range(lo, hi):
                        mm = nc.tensor.matmul(banks[n % len(banks)][:, (b - lo) * D:(b - lo + 1) * D],
                                              lhsT=xT_all[:, b * P:(b + 1) * P], rhs=w[:, :], start=True, stop=True)
                    mm.then_inc(tab_mm, 1)
                    n += 1
            pe.wait_ge(half, 4)
            nc.tensor.matmul(pmisc[:, 0:2 * D], lhsT=w2T[:, :], rhs=wa[:, :], start=True, stop=True)
            nc.tensor.matmul(pmisc[0:1, 2 * D:4 * D], lhsT=b2c[:, :], rhs=wa[:, :],
                             start=True, stop=True).then_inc(fold_mm, 1)
            pe.wait_ge(bad_ready, 1)
            pe.wait_ge(fold_ready, 2)
            nc.tensor.matmul(pmisc[0:1, 0:1], lhsT=bad[:, 3:4], rhs=ones[:, 0:1], start=True, stop=True).then_inc(bad_mm, 1)
            pe.wait_ge(flag_ready, 1)
            bad_v = pe.value_load(flag[0:1, 0:1], min_val=0, max_val=3 * P)

            def first(b):
                return isinstance(b, int) and b == 0

            def node_products(b, s, m):
                pe.wait_ge(*((xT_blk_in, b * 16 + 16) if s == 0 else (xT_last_in, 16 * len(ENDING))))
                if not fresh(m):
                    pe.wait_ge(xg_ready, b)
                nc.tensor.matmul(px[s][:, 0:2 * D], lhsT=xT_blk[s][:, :], rhs=wx[:, :], start=True, stop=True)
                pe.wait_ge(ablk_ready, b + 1)
                pe.wait_ge(cblk_ready, b + 1)
                if not fresh(m):
                    pe.wait_ge(gt_ready, b)
                nc.tensor.matmul(pa[s][:, 2 * D:2 * D + 1], lhsT=cblk[s][VR - 1:VR, :], rhs=ones[VR - 1:VR, 0:1],
                                 start=True, stop=True)
                nc.tensor.matmul(pa[s][:, 0:2 * D], lhsT=ablk[s][:, :], rhs=w2a[:, :], start=True, stop=False)
                nc.tensor.matmul(pa[s][:, 0:2 * D], lhsT=cblk[s][:, :], rhs=vec[:, :],
                                 start=False, stop=True).then_inc(node_mm, 1)

            def pre_products(i, j, off, k):
                pe.wait_ge(ohT_ready, i * NG + (j + 1))
                if not (isinstance(i, int) and i * NG + j < before(j)):
                    pe.wait_ge(h_ready, i * NG + (j + 1 - before(j)))
                for c in range(k):
                    mm = nc.tensor.matmul(pre[j % RING][:, c * D:(c + 1) * D], lhsT=lhs[:, j, c * P:(c + 1) * P],
                                          rhs=win[:, j, :], start=True, stop=True)
                mm.then_inc(pre_done, 1)

            def agg_products(i, j, off, k):
                pe.wait_ge(oh_ready, i * NG + (j + 1))
                pe.wait_ge(h_ready, i * NG + (j + 1))
                if not (isinstance(i, int) and i * NG + j < before(j)):
                    pe.wait_ge(added, i * NG + (j + 1 - before(j)))
                for c in range(k):
                    nc.tensor.matmul(pagg[j % RING][:, 0:WIN], lhsT=h[:, j % RING, c, :], rhs=onehot[:, j, c, :],
                                     start=(c == 0), stop=(c == k - 1))
                nc.tensor.matmul(pagg[j % RING][:, WIN:WIN + k * WIN], lhsT=ones[:, :],
                                 rhs=onehot[:, j, 0:k, :].rearrange("p c w -> p (c w)"),
                                 start=True, stop=True).then_inc(agg_done, 1)

            def body(i):
                for j, off, k in groups_of(i):
                    if near(i, j, 1):
                        pre_products(*near(i, j, 1))
                    if near(i, j, -1):
                        agg_products(*near(i, j, -1))
                    if j == 0 and not (isinstance(i, int) and i < 2):
                        node_products(*in_turn(i - 2))

            with pe.If(bad_v == 0):
                pre_products(*near(0, 0, 0))
                run_iterations(pe, body)
                agg_products(*near(ITERS, len(LAST) - 1, 0))
                for e in ENDING:
                    node_products(*e)
            with pe.Else():
                def sum_tile(t):
                    pe.wait_ge(g_ef, t * 16 + 16)
                    if not isinstance(t, int):
                        pe.wait_ge(g_sum, t)
                    nc.tensor.matmul(pre[0][:, 0:D], lhsT=sef[:, :], rhs=win[0:DE, 0, :],
                                     start=True, stop=True).then_inc(g_pre, 1)
                    pe.wait_ge(g_h, t + 1)
                    take_waits(pe)
                    with pe.Fori(0, NB) as b:
                        pe.wait_ge(g_oh, t * NB + b + 1)
                        nc.tensor.matmul(pagg[0][:, 0:P], lhsT=sh[:, :], rhs=soh[:, :], start=True, stop=True)
                        nc.tensor.matmul(pagg[0][:, P:2 * P], lhsT=ones[:, :], rhs=soh[:, :],
                                         start=True, stop=True).then_inc(g_mm, 1)
                sum_tile(0)
                with pe.Fori(1, NT) as t:
                    sum_tile(t)
                loop_blocks(pe, lambda b: node_products(*in_turn(b)))

        @block.vector
        def _(dve):
            def done(n):
                dve.wait_ge(prep, n)

            nc.vector.memset(ones[:, :], 1.0).then_inc(ones_ready, 1)
            nc.vector.memset(vec[:, :], 0.0).then_inc(vec_zero, 1)
            nc.vector.memset(aggcnt[:, :, :], 0.0).then_inc(prep, 1)
            dve.wait_ge(iota_ready, 2)
            nc.vector.tensor_copy(iota_f[:, :], iota_i[:, :]).then_inc(prep, 1)
            nc.vector.tensor_copy(node_f[:, :], node_i[:, :]).then_inc(prep, 1)
            dve.wait_ge(tab_in, 48)
            nc.vector.tensor_copy(base_f[:, :], base_i[:, :]).then_inc(prep, 1)
            nc.vector.tensor_copy(dst_f[:, :], dst_i[:, :]).then_inc(prep, 1)
            done(5)
            nc.vector.tensor_scalar(base_col[:, :], base_f[:, :], -1.0, node_f[:, 0:1], ALU.mult, ALU.add).then_inc(prep, 1)
            nc.vector.tensor_tensor(slack[:, :], base_f[:, :], open_i[:, :], ALU.subtract).then_inc(prep, 1)
            whole = ITERS * TILES
            d3 = dst_f[:, 0:whole].rearrange("p (i t) -> p i t", t=TILES)
            r3 = rel[:, 0:whole].rearrange("p (i t) -> p i t", t=TILES)
            b3 = base_f[:, 0:ITERS * BPI].rearrange("p (i g) -> p i g", g=BPI)
            for j in range(NG):
                o, k = OFFS[j], GROUPS[j]
                nc.vector.tensor_tensor(r3[:, :, o:o + k], d3[:, :, o:o + k],
                                        b3[:, :, j:j + 1].to_broadcast([P, ITERS, k]), ALU.subtract).then_inc(prep, 1)
            for j, (o, k) in enumerate(LAST):
                nc.vector.tensor_scalar(rel[:, whole + o:whole + o + k], dst_f[:, whole + o:whole + o + k],
                                        base_f[:, ITERS * BPI + j:ITERS * BPI + j + 1], None,
                                        ALU.subtract).then_inc(prep, 1)
            n = 7 + NG + len(LAST)
            done(n)
            nc.vector.tensor_reduce(red[:, 0:1], rel[:, :], AX.X, ALU.max).then_inc(prep, 1)
            nc.vector.tensor_reduce(red[:, 1:2], rel[:, :], AX.X, ALU.min).then_inc(prep, 1)
            nc.vector.tensor_reduce(red[:, 2:3], slack[:, :], AX.X, ALU.min).then_inc(prep, 1)
            done(n + 3)
            nc.vector.tensor_scalar(bad[:, 0:1], red[:, 0:1], float(WIN), None, ALU.is_ge).then_inc(prep, 1)
            nc.vector.tensor_scalar(bad[:, 1:3], red[:, 1:3], 0.0, None, ALU.is_lt).then_inc(prep, 1)
            done(n + 5)
            nc.vector.tensor_reduce(bad[:, 3:4], bad[:, 0:3], AX.X, ALU.add).then_inc(bad_ready, 1)
            dve.wait_ge(bc_in, 48)
            for c in range(NCH):
                lo, hi = c * XCH, min((c + 1) * XCH, NB)
                dve.wait_ge(tab_mm, NCH + c + 1)
                bk = banks[(NCH + c) % len(banks)][:, 0:(hi - lo) * D].rearrange("p (b f) -> p b f", f=D)
                b1v = b1_bc[:, :].rearrange("p (a f) -> p a f", a=1).to_broadcast([P, hi - lo, D])
                nc.vector.tensor_tensor(pst[:, 1, lo:hi, :], bk, b1v, ALU.add).then_inc(pdst_sb, 1)
            dve.wait_ge(bad_mm, 1)
            nc.vector.tensor_copy(flag[:, :], pmisc[0:1, 0:1]).then_inc(flag_ready, 1)
            dve.wait_ge(x_in, 16)
            dve.wait_ge(flag_ready, 1)
            bad_v = dve.value_load(flag[0:1, 0:1], min_val=0, max_val=3 * P)

            def first(b):
                return isinstance(b, int) and b == 0

            NEWTON = 3
            RS = 3 + 2 * NEWTON
            CHAIN = 11 + 2 * RS

            def after(s, m, n):
                dve.wait_ge(chain[s], m * CHAIN + n)

            def count_rows(b, s, m):
                if not fresh(m):
                    dve.wait_ge(node_mm, b)
                nc.vector.tensor_reduce(cblk[s][:, :], aggcnt[0:VR, 1:1 + KMAX, bass.ds(b * P, P)]
                                        .rearrange("p c n -> p n c"), AX.X, ALU.add).then_inc(cnt_ready, 1)
                dve.wait_ge(cnt_ready, b + 1)
                nc.vector.tensor_scalar(cblk[s][VR - 1:VR, :], cblk[s][VR - 1:VR, :], 1.0, None,
                                        ALU.max).then_inc(cblk_ready, 1)

            def gate_sum(blocks):
                for b, s, m in blocks:
                    dve.wait_ge(node_mm, b + 1)
                    nc.vector.reciprocal(rcp[s][:, :], pa[s][:, 2 * D:2 * D + 1]).then_inc(chain[s], 1)
                    after(s, m, 1)
                    dve.wait_ge(xg_ready, b + 1)
                    if not fresh(m):
                        dve.wait_ge(th_ready, b)
                    nc.vector.scalar_tensor_tensor(out=gt[s][:, :], in0=pa[s][:, 0:2 * D], scalar=rcp[s][:, :],
                                                   in1=xg[s][:, :], op0=ALU.mult, op1=ALU.add).then_inc(gt_ready, 1)

            def rsqrt(blocks, n):
                for b, s, m in blocks:
                    nc.vector.tensor_scalar(nt[s][:, 0:1], mv[s][:, 1:2], EPS, None, ALU.add).then_inc(chain[s], 1)
                for b, s, m in blocks:
                    after(s, m, n + 1)
                    nc.vector.tensor_scalar(nhv[s][:, :], nt[s][:, 0:1], -0.5, None, ALU.mult).then_inc(chain[s], 1)
                    nc.vector.tensor_scalar(yi[s][:, :], nt[s][:, 0:1].bitcast(I32), -0.5, float(0x5F3759DF),
                                            ALU.mult, ALU.add).then_inc(chain[s], 1)
                for step in range(NEWTON):
                    for b, s, m in blocks:
                        y = nt[s][:, 2:3] if step else yi[s][:, :].bitcast(F32)
                        after(s, m, n + 3 + 2 * step)
                        nc.vector.scalar_tensor_tensor(out=nt[s][:, 1:2], in0=y, scalar=y, in1=nhv[s][:, :],
                                                       op0=ALU.mult, op1=ALU.mult).then_inc(chain[s], 1)
                    for b, s, m in blocks:
                        y = nt[s][:, 2:3] if step else yi[s][:, :].bitcast(F32)
                        after(s, m, n + 4 + 2 * step)
                        nc.vector.scalar_tensor_tensor(out=nt[s][:, 2:3], in0=nt[s][:, 1:2], scalar=1.5, in1=y,
                                                       op0=ALU.add, op1=ALU.mult).then_inc(chain[s], 1)

            def moments(blocks, rows, n):
                for b, s, m in blocks:
                    after(s, m, n)
                    nc.vector.bn_stats(stats[s][:, :], rows[s][:, :]).then_inc(chain[s], 1)
                for b, s, m in blocks:
                    after(s, m, n + 1)
                    if not isinstance(b, int):
                        take_waits(dve)
                    nc.vector.bn_aggr(mv[s][:, :], stats[s][:, :]).then_inc(chain[s], 1)
                for b, s, m in blocks:
                    after(s, m, n + 2)

            def mix_in(blocks):
                for b, s, m in blocks:
                    dve.wait_ge(th_ready, b + 1)
                    xv = x_all[:, bass.ds(b, 1), :].rearrange("p a f -> p (a f)")
                    nc.vector.tensor_tensor(diff[s][:, :], xv, th[s][:, D:2 * D], ALU.subtract).then_inc(chain[s], 1)
                    nc.vector.tensor_tensor(xb[s][:, :], xv, beta_bc[:, :], ALU.add).then_inc(chain[s], 1)
                    after(s, m, 2)
                    nc.vector.scalar_tensor_tensor(out=mix[s][:, :], in0=th[s][:, 0:D], scalar=1.0, in1=diff[s][:, :],
                                                   op0=ALU.add, op1=ALU.mult).then_inc(chain[s], 1)
                    after(s, m, 4)
                    nc.vector.scalar_tensor_tensor(out=upd[s][:, :], in0=mix[s][:, :], scalar=0.5,
                                                   in1=th[s][:, D:2 * D], op0=ALU.mult, op1=ALU.add).then_inc(upd_ready, 1)
                    dve.wait_ge(upd_ready, b + 1)
                moments(blocks, upd, 4)

            def norm_in(blocks):
                rsqrt(blocks, 6)
                n = 6 + RS
                for b, s, m in blocks:
                    after(s, m, n)
                    nc.vector.tensor_scalar(nrm[s][:, :], upd[s][:, :], mv[s][:, 0:1], nt[s][:, 2:3], ALU.subtract,
                                            ALU.mult).then_inc(chain[s], 1)
                for b, s, m in blocks:
                    after(s, m, n + 1)
                    nc.vector.tensor_tensor(ynew[s][:, :], nrm[s][:, :], gamma_bc[:, :], ALU.mult).then_inc(chain[s], 1)
                for b, s, m in blocks:
                    after(s, m, n + 2)
                    nc.vector.tensor_tensor(ysum[s][:, :], ynew[s][:, :], xb[s][:, :], ALU.add).then_inc(chain[s], 1)

            def norm_out(blocks):
                n = 9 + RS
                moments(blocks, ysum, n)
                rsqrt(blocks, n + 2)
                for b, s, m in blocks:
                    after(s, m, CHAIN)
                    if not fresh(m):
                        dve.wait_ge(out_done, b * 16)
                    nc.vector.tensor_scalar(oblk[s][:, :], ysum[s][:, :], mv[s][:, 0:1], nt[s][:, 2:3], ALU.subtract,
                                            ALU.mult).then_inc(out_ready, 1)

            def prepare(i, j, off, k):
                if not (isinstance(i, int) and i == 0):
                    dve.wait_ge(agg_done, i * NG + (j + 1 - NG))
                i0 = iota_f[:, 0:WIN].rearrange("p (a w) -> p a w", a=1).to_broadcast([P, k, WIN])
                r0 = rel[:, bass.ds(i * TILES + off, k)].rearrange("p (k a) -> p k a", a=1).to_broadcast([P, k, WIN])
                nc.vector.tensor_tensor(onehot[:, j, 0:k, :], i0, r0, ALU.is_equal).then_inc(oh_ready, 1)

            def add_rows(i, j, k):
                dve.wait_ge(pre_done, i * NG + (j + 1))
                dve.wait_ge(gath_in[j], i * (16 * k) + 16 * k if not (isinstance(i, int) and i == ITERS)
                            else ITERS * 16 * GROUPS[j] + 16 * k)
                z = pre[j % RING][:, 0:k * D].rearrange("p (c f) -> p c f", f=D)
                nc.vector.tensor_tensor(z, z, gath[:, j, 0:k, :], ALU.add).then_inc(sum_done, 1)

            def add_window(i, j, off, k):
                base = load_base(dve, i, j)
                dve.wait_ge(agg_done, i * NG + (j + 1))
                if not (isinstance(i, int) and i * NG + j == 0):
                    dve.wait_ge(added, i * NG + j)
                w = aggcnt[:, 0:1 + k, bass.ds(base, WIN)]
                nc.vector.tensor_tensor(w, w, pagg[j % RING][:, 0:WIN + k * WIN].rearrange("p (a w) -> p a w", w=WIN),
                                        ALU.add).then_inc(added, 1)

            def body(i):
                older = not (isinstance(i, int) and i < 2)
                for j, off, k in groups_of(i):
                    if near(i, j, 1):
                        prepare(*near(i, j, 1))
                    if near(i, j, -2):
                        add_window(*near(i, j, -2))
                    if j == NG - 1 and not first(i):
                        dve.wait_ge(added, i * NG + AHEAD)
                        count_rows(*in_turn(i - 1))
                    add_rows(i, j, k)
                    if older and j == 1:
                        gate_sum([in_turn(i - 2)])
                    if older and j == 2:
                        mix_in([in_turn(i - 2)])
                    if older and j == 3:
                        norm_in([in_turn(i - 2)])
                    if older and j == 4:
                        norm_out([in_turn(i - 2)])

            with dve.If(bad_v == 0):
                prepare(*near(0, 0, 0))
                run_iterations(dve, body)
                mix_in([in_turn(ITERS - 2)])
                norm_in([in_turn(ITERS - 2)])
                norm_out([in_turn(ITERS - 2)])
                for d in (-1, 0):
                    add_window(*near(ITERS, len(LAST) - 1, d))
                dve.wait_ge(added, ITERS * NG + len(LAST))
                for e in ENDING:
                    count_rows(*e)
                for e in ENDING:
                    gate_sum([e])
                mix_in(ENDING)
                norm_in(ENDING)
                norm_out(ENDING)
            with dve.Else():
                def sum_tile(t):
                    dve.wait_ge(g_pre, t + 1)
                    dve.wait_ge(g_gath, t * 32 + 32)
                    if not isinstance(t, int):
                        dve.wait_ge(g_h, t)
                    nc.vector.tensor_tensor(pre[1][:, 0:D], pre[0][:, 0:D], sgath[:, 0, :], ALU.add).then_inc(g_sum0, 1)
                    dve.wait_ge(g_sum0, t + 1)
                    nc.vector.tensor_tensor(pre[1][:, 0:D], pre[1][:, 0:D], sgath[:, 1, :], ALU.add).then_inc(g_sum, 1)
                    if not isinstance(t, int):
                        dve.wait_ge(g_oh, t * NB)
                    nc.vector.tensor_copy(shift[:, :], dst_f[:, bass.ds(t, 1)]).then_inc(g_shift, 1)
                    with dve.Fori(0, NB) as b:
                        dve.wait_ge(g_shift, t * (NB + 1) + b + 1)
                        nc.vector.tensor_scalar(soh[:, :], iota_f[:, :], shift[:, 0:1], None,
                                                ALU.is_equal).then_inc(g_oh, 1)
                        dve.wait_ge(g_oh, t * NB + b + 1)
                        nc.vector.tensor_scalar(shift[:, :], shift[:, :], float(P), None,
                                                ALU.subtract).then_inc(g_shift, 1)
                        dve.wait_ge(g_mm, t * NB + b + 1)
                        w = aggcnt[:, 0:2, bass.ds(b * P, P)]
                        nc.vector.tensor_tensor(w, w, pagg[0][:, 0:2 * P].rearrange("p (a w) -> p a w", a=2),
                                                ALU.add).then_inc(g_added, 1)
                    dve.wait_ge(g_added, t * NB + NB)
                sum_tile(0)
                with dve.Fori(1, NT) as t:
                    sum_tile(t)

                def stage(b):
                    count_rows(*in_turn(b))
                    gate_sum([in_turn(b)])
                    mix_in([in_turn(b)])
                    norm_in([in_turn(b)])
                    norm_out([in_turn(b)])
                loop_blocks(dve, stage)


def kernel(x, src, dst, edge_attr_64, L0_gnn_W1, L0_gnn_b1, L0_gnn_W2, L0_gnn_b2, L0_gnn_Wg, L0_gnn_bg,
           L0_gnn_Wt, L0_gnn_bt, L0_gnn_gamma, L0_gnn_beta):
    import concourse.bacc as _bacc
    from concourse.bass_utils import run_bass_kernel_spmd as _run

    x, src, dst, ef = (np.asarray(a) for a in (x, src, dst, edge_attr_64))
    n, e = x.shape[0], src.shape[0]
    nb, nt, iters, last = shapes(n, e)
    src_p = np.concatenate([src, np.zeros((iters + 1) * TILES * P - e, src.dtype)])
    dst_p = np.concatenate([dst, np.full(nt * P - e, n, dst.dtype)])
    x_p = np.concatenate([x, np.zeros((nb * P - n, D), x.dtype)])
    ef_p = np.concatenate([ef, np.zeros((nt * P - e, DE), ef.dtype)])
    starts, opened = np.zeros((iters + 1, BPI), np.int64), np.zeros((iters + 1, BPI), np.int32)
    for i in range(iters + 1):
        offs = OFFS if i < iters else [o for o, _ in last]
        for j in range(BPI):
            jj = min(j, len(offs) - 1)
            starts[i, j] = (i * TILES + offs[jj]) * P
            opened[i, j] = P * max(i if jj >= AHEAD else i - 1, 0)
    arrays = {
        "x": x_p, "xT": x_p.T, "src_pt": src_p.reshape(-1, P).T, "dst_pt": dst_p.reshape(nt, P).T,
        "dst_flat": dst_p.reshape(1, -1), "base_tab": dst_p[starts.ravel()].reshape(1, -1),
        "open_tab": opened.reshape(1, -1), "efT": ef_p.T,
        "W1": L0_gnn_W1, "b1": np.asarray(L0_gnn_b1).reshape(1, -1), "W2T": np.asarray(L0_gnn_W2).T,
        "b2": np.asarray(L0_gnn_b2).reshape(-1, 1), "Wg": L0_gnn_Wg, "bg": np.asarray(L0_gnn_bg).reshape(1, -1),
        "Wt": L0_gnn_Wt, "bt": np.asarray(L0_gnn_bt).reshape(1, -1),
        "gamma": np.asarray(L0_gnn_gamma).reshape(1, -1), "beta": np.asarray(L0_gnn_beta).reshape(1, -1),
    }
    arrays = {f"in_{k}": np.ascontiguousarray(v) for k, v in arrays.items()}
    nc = _bacc.Bacc("TRN2", target_bir_lowering=False, num_devices=1)
    args = [nc.dram_tensor(k, v.shape, mybir.dt.from_np(v.dtype), kind="ExternalInput").ap() for k, v in arrays.items()]
    out = nc.dram_tensor("out_x", (n, D), F32, kind="ExternalOutput").ap()
    gnn_kernel(nc, *args, out)
    r = _run(nc, [arrays], core_ids=[0])
    return r.results[0]["out_x"]
```

```python
from contextlib import ExitStack

import numpy as np
import concourse.bass as bass
from concourse import mybir

ALU = mybir.AluOpType
ACT = mybir.ActivationFunctionType
AX = mybir.AxisListType
F32 = mybir.dt.float32
I32 = mybir.dt.int32

P = 128
D = 128
DE = 64
WIN = 64
EPS = 1e-5

NG = 4
GT = 4
TILES = NG * GT
LAG = 2
CLOSE = 3
VR = 33


def shapes(n_nodes, n_edges):
    blocks = -(-n_nodes // P)
    iters = -(-n_edges // (TILES * P))
    assert iters - LAG == blocks - 1 and iters >= 6
    return blocks, iters * TILES, iters


def gnn_kernel(nc, x, xT, src_pt, dst_pt, dst_flat, base_tab, open_tab, efT,
               W1, b1, W2T, b2, Wg, bg, Wt, bt, gamma, beta, out):
    N = out.shape[0]
    NP = x.shape[0]
    NB, NT, ITERS = shapes(N, dst_pt.shape[1] * P)
    FINAL = ITERS - 1
    assert NP == NB * P and D == P
    NBASE = base_tab.shape[1]
    ROWS_LAST = N - (NB - 1) * P
    SUMS = 2
    LAST = NB - 1
    LAST_S = 1
    NS = 2

    with ExitStack() as ctx:
        def sb(name, shape, dt=F32):
            return ctx.enter_context(nc.sbuf_tensor(name, shape, dt))

        def ps(name, shape):
            return ctx.enter_context(nc.psum_tensor(name, shape, F32))

        def sem(name):
            return ctx.enter_context(nc.semaphore(name))

        psrc_d = nc.dram_tensor("psrc_d", [NP, D], F32).ap()
        pdst_d = nc.dram_tensor("pdst_d", [NP, D], F32).ap()

        xT_all = sb("xT_all", [P, NP])
        x_all = sb("x_all", [P, NB, D])
        w1s = sb("w1s", [P, D])
        w1d = sb("w1d", [P, D])
        w2T = sb("w2T", [P, D])
        wx = sb("wx", [P, 2 * D])
        wa = sb("wa", [P, 2 * D])
        w2a = sb("w2a", [P, 2 * D])
        b2c = sb("b2c", [P, 1])
        vec = sb("vec", [VR, 2 * D])
        b1_bc = sb("b1_bc", [P, D])
        gamma_bc = sb("gamma_bc", [P, D])
        beta_bc = sb("beta_bc", [P, D])
        ones = sb("ones", [P, P])
        iota_i = sb("iota_i", [P, P], I32)
        iota_f = sb("iota_f", [P, P])
        node_i = sb("node_i", [P, 1], I32)
        node_f = sb("node_f", [P, 1])
        ident = sb("ident", [P, P])
        src_i = sb("src_i", [P, src_pt.shape[1]], I32)
        dst_i = sb("dst_i", [P, NT], I32)
        base_i = sb("base_i", [P, NBASE], I32)
        open_i = sb("open_i", [P, NBASE], I32)
        base_f = sb("base_f", [P, NBASE])
        base_col = sb("base_col", [P, NBASE])
        slack = sb("slack", [P, NBASE])
        rel = sb("rel", [P, NT])
        dst_f = sb("dst_f", [P, NT])
        red = sb("red", [P, 4])
        bad = sb("bad", [P, 4])
        flag = sb("flag", [1, 1], I32)
        aggcnt = sb("aggcnt", [P, 1 + GT, NP])
        pst = sb("pst", [P, 2, NB, D])

        idx = sb("idx", [P, NG, GT], I32)
        lhs = sb("lhs", [P, NG, GT * P])
        dstb = sb("dstb", [P, NG, GT * P], I32)
        win = sb("win", [P, NG, D])
        gath = sb("gath", [P, NG, GT, D])
        onehot = sb("onehot", [P, NG, GT, WIN])
        h = sb("h", [P, NG, GT, D])

        xT_blk = [sb(f"xT_blk{s}", [P, P]) for s in range(NS)]
        ablk = [sb(f"ablk{s}", [P, P]) for s in range(NS)]
        cblk = [sb(f"cblk{s}", [VR, P]) for s in range(NS)]
        xg = [sb(f"xg{s}", [P, 2 * D]) for s in range(NS)]
        gt = [sb(f"gt{s}", [P, 2 * D]) for s in range(NS)]
        th = [sb(f"th{s}", [P, 2 * D]) for s in range(NS)]
        rcp = [sb(f"rcp{s}", [P, 1]) for s in range(NS)]
        diff = [sb(f"diff{s}", [P, D]) for s in range(NS)]
        mix = [sb(f"mix{s}", [P, D]) for s in range(NS)]
        upd = [sb(f"upd{s}", [P, D]) for s in range(NS)]
        xb = [sb(f"xb{s}", [P, D]) for s in range(NS)]
        nrm = [sb(f"nrm{s}", [P, D]) for s in range(NS)]
        ysum = [sb(f"ysum{s}", [P, D]) for s in range(NS)]
        ynew = [sb(f"ynew{s}", [P, D]) for s in range(NS)]
        stats = [sb(f"stats{s}", [P, 6]) for s in range(NS)]
        mv = [sb(f"mv{s}", [P, 2]) for s in range(NS)]
        nhv = [sb(f"nhv{s}", [P, 1]) for s in range(NS)]
        yi = [sb(f"yi{s}", [P, 1], I32) for s in range(NS)]
        nt = [sb(f"nt{s}", [P, 4]) for s in range(NS)]
        oblk = [sb(f"oblk{s}", [P, D]) for s in range(NS)]

        sidx = sb("sidx", [P, 2], I32)
        sef = sb("sef", [DE, P])
        sgath = sb("sgath", [P, 2, D])
        sh = sb("sh", [P, D])
        shift = sb("shift", [P, 1])
        soh = sb("soh", [P, P])

        pre = [ps(f"pre{j}", [P, GT * D]) for j in range(NG)]
        pagg = [ps(f"pagg{r}", [P, 512]) for r in range(SUMS)]
        pnx = ps("pnx", [P, 512])
        pna = ps("pna", [P, 512])
        pflag = pagg[1]
        pfold = pna
        px = [pnx, pre[0]]
        pa = [pna, pre[1]]
        turned = [pnx, pna]
        banks = pre + pagg[0:1]

        XCH = 4
        NCH = -(-NB // XCH)
        STORES = ((0, 3), (3, 5), (5, NCH))
        w1s_in = sem("w1s_in")
        w1d_in = sem("w1d_in")
        xT_in = [sem(f"xT_in{c}") for c in range(NCH)]
        tab_in = sem("tab_in")
        wgt_in = sem("wgt_in")
        b1_in = sem("b1_in")
        bc_in = sem("bc_in")
        src_in = sem("src_in")
        win_in = sem("win_in")
        ones_ready = sem("ones_ready")
        iota_ready = sem("iota_ready")
        tab_mm = sem("tab_mm")
        psrc_sb = sem("psrc_sb")
        pdst_sb = sem("pdst_sb")
        psrc_out = sem("psrc_out")
        pdst_out = sem("pdst_out")
        prep = sem("prep")
        PREP = 13
        bad_ready = sem("bad_ready")
        bad_mm = sem("bad_mm")
        flag_ready = sem("flag_ready")
        vec_zero = sem("vec_zero")
        half = sem("half")
        fold_mm = sem("fold_mm")
        fold_ready = sem("fold_ready")
        edges_in = [sem(f"edges_in{j}") for j in range(NG)]
        window_in = [sem(f"window_in{j}") for j in range(NG)]
        gath_in = [sem(f"gath_in{j}") for j in range(NG)]
        idx_ready = sem("idx_ready")
        turn_done = sem("turn_done")
        rowsT_ready = sem("rowsT_ready")
        away_ready = sem("away_ready")
        ohT_ready = sem("ohT_ready")
        oh_ready = sem("oh_ready")
        pre_done = sem("pre_done")
        sum_done = sem("sum_done")
        h_ready = sem("h_ready")
        zero_ready = sem("zero_ready")
        agg_done = sem("agg_done")
        added = sem("added")
        passed = sem("passed")
        blk_in = [sem(f"blk_in{s}") for s in range(NS)]
        ablk_ready = sem("ablk_ready")
        node_x_mm = sem("node_x_mm")
        node_mm = sem("node_mm")
        xg_ready = sem("xg_ready")
        gt_ready = sem("gt_ready")
        th_ready = sem("th_ready")
        upd_ready = sem("upd_ready")
        chain = [sem(f"chain{s}") for s in range(NS)]
        cnt_ready = sem("cnt_ready")
        cblk_ready = sem("cblk_ready")
        out_ready = sem("out_ready")
        out_done = sem("out_done")
        g_idx_half = sem("g_idx_half")
        g_idx = sem("g_idx")
        g_ef = sem("g_ef")
        g_gath = sem("g_gath")
        g_pre = sem("g_pre")
        g_sum0 = sem("g_sum0")
        g_sum = sem("g_sum")
        g_h = sem("g_h")
        g_shift = sem("g_shift")
        g_oh = sem("g_oh")
        g_mm = sem("g_mm")
        g_added = sem("g_added")

        block = ctx.enter_context(nc.Block())

        def first(b):
            return isinstance(b, int) and b == 0

        def in_turn(b):
            return (b, 0, b)

        ENDING = (LAST, LAST_S, 0)

        def take_waits(eng):
            eng.sem_inc(passed, 1)

        def near(i, j, d):
            up, jj = divmod(j + d, NG)
            ii = i + up if up else i
            if isinstance(ii, int) and not 0 <= ii < ITERS:
                return None
            return ii, jj

        def closed(i, back=0):
            b = i - (LAG + back)
            return None if isinstance(b, int) and b < 0 else b

        def run_iterations(eng, body, between={}):
            for i in range(LAG + 3):
                if i in between:
                    between[i]()
                body(i)
            with eng.Fori(LAG + 3, FINAL) as i:
                body(i)
            body(FINAL)

        def load_edges(eng, i, j):
            e0 = (i * TILES + j * GT) * P
            eng.dma_start(dstb[DE:P, j, :],
                          dst_flat[0:1, bass.ds(e0, GT * P)].to_broadcast([WIN, GT * P])).then_inc(edges_in[j], 16)
            eng.dma_start(lhs[0:DE, j, :], efT[:, bass.ds(e0, GT * P)]).then_inc(edges_in[j], 16)

        def load_base(eng, i, j):
            return eng.value_load(base_i[0:1, bass.ds(i * NG + j, 1)], min_val=0, max_val=N)

        def loop_blocks(eng, stage):
            stage(0)
            with eng.Fori(1, NB - 1) as b:
                stage(b)
            stage(NB - 1)

        @block.sync
        def _(sp):
            sp.dma_start(w1s[:, :], W1[0:D, :]).then_inc(w1s_in, 16)
            for c in range(NCH):
                lo, hi = c * XCH * P, min((c + 1) * XCH, NB) * P
                sp.dma_start(xT_all[:, lo:hi], xT[:, lo:hi]).then_inc(xT_in[c], 16)
            sp.dma_start(w1d[:, :], W1[D:2 * D, :]).then_inc(w1d_in, 16)
            sp.dma_start(b1_bc[:, :], b1.to_broadcast([P, D])).then_inc(b1_in, 16)
            sp.dma_start(win[0:DE, :, :], W1[2 * D:2 * D + DE, :].rearrange("k (a n) -> k a n", a=1)
                         .to_broadcast([DE, NG, D])).then_inc(win_in, 16)
            for t, (table, ready, sent) in enumerate(((psrc_d, psrc_sb, psrc_out), (pdst_d, pdst_sb, pdst_out))):
                for c0, c1 in STORES:
                    lo, hi = c0 * XCH, min(c1 * XCH, NB)
                    sp.wait_ge(ready, c1)
                    sp.dma_start(table.rearrange("(b p) f -> p b f", p=P)[:, lo:hi, :],
                                 pst[:, t, lo:hi, :]).then_inc(sent, 16)

            def block_load(b, s=0):
                if not first(b) and s == 0:
                    sp.wait_ge(node_x_mm, b)
                sent = blk_in[s]
                sp.dma_start(xT_blk[s][:, :], xT[:, bass.ds(b * P, P)]).then_inc(sent, 16)
                sp.dma_start(x_all[:, bass.ds(b, 1), :].rearrange("p a f -> p (a f)"),
                             x[bass.ds(b * P, P), :]).then_inc(sent, 16)

            def body(i):
                for j in range(NG):
                    if not first(i):
                        sp.wait_ge(pre_done, i * NG + (j - NG + 1))
                    base = load_base(sp, i, j)
                    if not first(i):
                        load_edges(sp, i, j)
                    if first(i) and j == 0:
                        sp.wait_ge(pdst_out, 16 * len(STORES))
                    sp.dma_start(win[DE:P, j, :], pdst_d[bass.ds(base, WIN), :]).then_inc(window_in[j], 16)
                    if j == 1 and closed(i, 1) is not None:
                        block_load(closed(i, 1))

            sp.wait_ge(win_in, 16)
            sp.wait_ge(flag_ready, 1)
            bad_v = sp.value_load(flag[0:1, 0:1], min_val=0, max_val=3 * P)
            with sp.If(bad_v == 0):
                run_iterations(sp, body)
                block_load(LAST - 1)
                block_load(LAST, LAST_S)
            with sp.Else():
                def load_tile(t):
                    if not isinstance(t, int):
                        sp.wait_ge(g_pre, t)
                    sp.dma_start(sef[:, :], efT[:, bass.ds(t * P, P)]).then_inc(g_ef, 16)
                load_tile(0)
                with sp.Fori(1, NT) as t:
                    load_tile(t)

                loop_blocks(sp, block_load)
            sp.wait_ge(out_done, 16 * NB)

        @block.gpsimd
        def _(pool):
            nc.gpsimd.iota(iota_i[:, :], pattern=[[1, P]], base=0, channel_multiplier=0).then_inc(iota_ready, 1)
            nc.gpsimd.iota(node_i[:, :], pattern=[[0, 1]], base=WIN, channel_multiplier=-1).then_inc(iota_ready, 1)
            pool.wait_ge(src_in, 16)
            for j in range(NG):
                for c in range(GT):
                    nc.gpsimd.indirect_dma_start(
                        out=gath[:, j, c, :], out_offset=None, in_=x,
                        in_offset=bass.IndirectOffsetOnAxis(ap=src_i[:, j * GT + c:j * GT + c + 1], axis=0)
                    ).then_inc(gath_in[j], 16)
            pool.wait_ge(flag_ready, 1)
            bad_v = pool.value_load(flag[0:1, 0:1], min_val=0, max_val=3 * P)

            def body(i):
                if first(i):
                    return
                for j in range(NG):
                    if isinstance(i, int) and i == 1:
                        pool.wait_ge(idx_ready, 1)
                        pool.wait_ge(turn_done, j + 1)
                    else:
                        pool.wait_ge(idx_ready, i * NG + (j + 2 - 2 * NG))
                        pool.wait_ge(sum_done, i * NG + (j + 1 - 2 * NG))
                        take_waits(pool)
                    for c in range(GT):
                        nc.gpsimd.indirect_dma_start(
                            out=gath[:, j, c, :], out_offset=None, in_=psrc_d,
                            in_offset=bass.IndirectOffsetOnAxis(ap=idx[:, j, c:c + 1], axis=0)).then_inc(gath_in[j], 16)

            pool.wait_ge(psrc_out, 16 * len(STORES))
            with pool.If(bad_v == 0):
                run_iterations(pool, body)
            with pool.Else():
                pool.wait_ge(pdst_out, 16 * len(STORES))

                def gather_tile(t):
                    pool.wait_ge(g_idx, t + 1)
                    if not isinstance(t, int):
                        pool.wait_ge(g_sum, t)
                        take_waits(pool)
                    for c, table in enumerate((psrc_d, pdst_d)):
                        nc.gpsimd.indirect_dma_start(
                            out=sgath[:, c, :], out_offset=None, in_=table,
                            in_offset=bass.IndirectOffsetOnAxis(ap=sidx[:, c:c + 1], axis=0)).then_inc(g_gath, 16)
                gather_tile(0)
                with pool.Fori(1, NT) as t:
                    gather_tile(t)

        @block.scalar
        def _(act):
            act.dma_start(src_i[:, :], src_pt).then_inc(src_in, 16)
            act.dma_start(dst_i[:, :], dst_pt).then_inc(tab_in, 16)
            act.dma_start(base_i[:, :], base_tab.to_broadcast([P, NBASE])).then_inc(tab_in, 16)
            act.dma_start(open_i[:, :], open_tab.to_broadcast([P, NBASE])).then_inc(tab_in, 16)
            act.wait_ge(ones_ready, 1)
            nc.scalar.activation(sh[:, 0:1], ones[:, 0:1], ACT.Silu).then_inc(half, 1)
            act.wait_ge(src_in, 16)
            nc.scalar.activation(idx[:, :, :], src_i[:, TILES:2 * TILES].rearrange("p (j c) -> p j c", c=GT),
                                 ACT.Copy).then_inc(idx_ready, 1)
            for lane in range(GT):
                nc.scalar.activation(aggcnt[:, lane, :].rearrange("p (b f) -> p b f", f=P),
                                     ones[:, :].rearrange("p (a f) -> p a f", a=1).to_broadcast([P, NB, P]),
                                     ACT.Copy, scale=0.0).then_inc(zero_ready, 1)
                if lane == 1:
                    for j in range(NG):
                        load_edges(act, 0, j)

            def load_weights():
                act.wait_ge(vec_zero, 1)
                for dst_ap, src_ap in ((wx[:, 0:D], Wg[0:D, :]), (wx[:, D:2 * D], Wt[0:D, :]),
                                       (wa[:, 0:D], Wg[D:2 * D, :]), (wa[:, D:2 * D], Wt[D:2 * D, :]),
                                       (vec[VR - 1:VR, 0:D], bg), (vec[VR - 1:VR, D:2 * D], bt),
                                       (w2T[:, :], W2T), (b2c[:, :], b2)):
                    act.dma_start(dst_ap, src_ap).then_inc(wgt_in, 16)
                act.dma_start(gamma_bc[:, :], gamma.to_broadcast([P, D])).then_inc(bc_in, 16)
                act.dma_start(beta_bc[:, :], beta.to_broadcast([P, D])).then_inc(bc_in, 16)

            def halve():
                act.wait_ge(wgt_in, 16 * 8)
                for w in (wx[:, 0:D], wa[:, 0:D], vec[VR - 1:VR, 0:D]):
                    nc.scalar.activation(w, w, ACT.Copy, scale=0.5).then_inc(half, 1)

            def keep_fold():
                act.wait_ge(fold_mm, 1)
                nc.scalar.activation(w2a[:, :], pfold[:, 0:2 * D], ACT.Copy).then_inc(fold_ready, 1)
                nc.scalar.activation(vec[0:1, :], pfold[0:1, 2 * D:4 * D], ACT.Copy).then_inc(fold_ready, 1)

            act.wait_ge(flag_ready, 1)
            bad_v = act.value_load(flag[0:1, 0:1], min_val=0, max_val=3 * P)

            def stage_copy(b, s, m):
                if not first(m):
                    act.wait_ge(node_mm, b)
                nc.scalar.activation(ablk[s][:, :], aggcnt[:, 0, bass.ds(b * P, P)], ACT.Copy).then_inc(ablk_ready, 1)

            def stage_xg(b, s, m):
                act.wait_ge(node_x_mm, b + 1)
                if not first(m):
                    act.wait_ge(gt_ready, b)
                nc.scalar.activation(xg[s][:, :], px[s][:, 0:2 * D], ACT.Copy).then_inc(xg_ready, 1)

            def stage_tanh(b, s, m):
                act.wait_ge(gt_ready, b + 1)
                if not first(m):
                    act.wait_ge(upd_ready, b)
                nc.scalar.activation(th[s][:, :], gt[s][:, :], ACT.Tanh).then_inc(th_ready, 1)

            def out_store(b, s):
                act.wait_ge(out_ready, b + 1)
                if isinstance(b, int) and b == LAST:
                    act.dma_start(out[b * P:N, :], oblk[s][0:ROWS_LAST, :]).then_inc(out_done, 16)
                else:
                    act.dma_start(out[bass.ds(b * P, P), :], oblk[s][:, :]).then_inc(out_done, 16)

            def onehot_T(i, j):
                act.wait_ge(edges_in[j], i * 32 + 32)
                nc.scalar.activation(lhs[DE:P, j, :], dstb[DE:P, j, :], ACT.Abs,
                                     bias=base_col[DE:P, bass.ds(i * NG + j, 1)]).then_inc(away_ready, 1)
                act.wait_ge(away_ready, i * NG + (j + 1))
                nc.scalar.activation(lhs[DE:P, j, :], lhs[DE:P, j, :], ACT.Relu, bias=1.0,
                                     scale=-1.0).then_inc(ohT_ready, 1)

            def next_idx(i, j):
                act.wait_ge(gath_in[j], i * (16 * GT) + 16 * GT)
                nc.scalar.activation(idx[:, j, :], src_i[:, bass.ds(i * TILES + (TILES + j * GT), GT)],
                                     ACT.Copy).then_inc(idx_ready, 1)

            def silu(i, j):
                if first(i):
                    act.wait_ge(pre_done, j + 1)
                else:
                    act.wait_ge(sum_done, i * NG + (j + 1 - NG))
                    act.wait_ge(agg_done, i * NG + (j + 1 - NG))
                nc.scalar.activation(h[:, j, :, :], pre[j][:, :].rearrange("p (c f) -> p c f", f=D),
                                     ACT.Silu).then_inc(h_ready, 1)

            def body(i):
                for j in range(NG):
                    if not (isinstance(i, int) and (i in (0, FINAL) or i == 1 and j == 0)):
                        next_idx(i, j)
                    silu(i, j)
                    if j == CLOSE and closed(i) is not None:
                        act.wait_ge(added, i * NG + CLOSE)
                        stage_copy(*in_turn(closed(i)))
                    if first(i) and j == NG - 1:
                        next_idx(1, 0)
                    if near(i, j, 3) and not first(near(i, j, 3)[0]):
                        onehot_T(*near(i, j, 3))
                    if j == 3 and closed(i) is not None:
                        stage_xg(*in_turn(closed(i)))
                    if j == 0 and closed(i, 1) is not None:
                        stage_tanh(*in_turn(closed(i, 1)))
                    if j == 1 and closed(i, 2) is not None:
                        out_store(closed(i, 2), 0)

            with act.If(bad_v == 0):
                for j in range(NG):
                    onehot_T(0, j)
                load_weights()
                run_iterations(act, body, {2: halve, 3: keep_fold})
                stage_xg(*ENDING)
                act.wait_ge(added, ITERS * NG)
                stage_copy(*ENDING)
                stage_tanh(*in_turn(LAST - 1))
                out_store(LAST - 2, 0)
                stage_tanh(*ENDING)
                out_store(LAST - 1, 0)
                out_store(LAST, LAST_S)
            with act.Else():
                load_weights()
                halve()
                keep_fold()

                def idx_tile(t):
                    if not isinstance(t, int):
                        act.wait_ge(g_gath, 32 * t)
                    nc.scalar.activation(sidx[:, 0:1], src_i[:, bass.ds(t, 1)], ACT.Copy).then_inc(g_idx_half, 1)
                    nc.scalar.activation(sidx[:, 1:2], dst_i[:, bass.ds(t, 1)], ACT.Copy).then_inc(g_idx, 1)
                    act.wait_ge(g_sum, t + 1)
                    if not isinstance(t, int):
                        act.wait_ge(g_mm, t * NB)
                    nc.scalar.activation(sh[:, :], pre[1][:, 0:D], ACT.Silu).then_inc(g_h, 1)
                idx_tile(0)
                with act.Fori(1, NT) as t:
                    idx_tile(t)
                act.wait_ge(g_added, NT * NB)

                def stage(b):
                    stage_copy(*in_turn(b))
                    stage_xg(*in_turn(b))
                    stage_tanh(*in_turn(b))
                    out_store(b, 0)
                loop_blocks(act, stage)

        @block.tensor
        def _(pe):
            n = 0
            for w, w_in in ((w1s, w1s_in), (w1d, w1d_in)):
                pe.wait_ge(w_in, 16)
                for c in range(NCH):
                    lo, hi = c * XCH, min((c + 1) * XCH, NB)
                    if w is w1s:
                        pe.wait_ge(xT_in[c], 16)
                    if n >= len(banks):
                        m = n - len(banks)
                        pe.wait_ge(*((psrc_sb, m + 1) if m < NCH else (pdst_sb, m - NCH + 1)))
                    for b in range(lo, hi):
                        mm = nc.tensor.matmul(banks[n % len(banks)][:, (b - lo) * D:(b - lo + 1) * D],
                                              lhsT=xT_all[:, b * P:(b + 1) * P], rhs=w[:, :], start=True, stop=True)
                    mm.then_inc(tab_mm, 1)
                    n += 1
                if w is w1s:
                    pe.wait_ge(bad_ready, 1)
                    nc.tensor.matmul(pflag[0:1, 0:1], lhsT=bad[:, 3:4], rhs=ones[:, 0:1],
                                     start=True, stop=True).then_inc(bad_mm, 1)

            def fold():
                pe.wait_ge(half, 4)
                nc.tensor.matmul(pfold[:, 0:2 * D], lhsT=w2T[:, :], rhs=wa[:, :], start=True, stop=True)
                nc.tensor.matmul(pfold[0:1, 2 * D:4 * D], lhsT=b2c[:, :], rhs=wa[:, :],
                                 start=True, stop=True).then_inc(fold_mm, 1)

            pe.wait_ge(flag_ready, 1)
            bad_v = pe.value_load(flag[0:1, 0:1], min_val=0, max_val=3 * P)

            def node_x(b, s, m):
                pe.wait_ge(blk_in[s], m * 32 + 32)
                if not first(m):
                    pe.wait_ge(xg_ready, b)
                nc.tensor.matmul(px[s][:, 0:2 * D], lhsT=xT_blk[s][:, :], rhs=wx[:, :],
                                 start=True, stop=True).then_inc(node_x_mm, 1)

            def node_agg(b, s, m):
                if isinstance(b, int):
                    pe.wait_ge(fold_ready, 2)
                pe.wait_ge(ablk_ready, b + 1)
                pe.wait_ge(cblk_ready, b + 1)
                if not first(m):
                    pe.wait_ge(gt_ready, b)
                nc.tensor.matmul(pa[s][:, 2 * D:2 * D + 1], lhsT=cblk[s][VR - 1:VR, :], rhs=ones[VR - 1:VR, 0:1],
                                 start=True, stop=True)
                nc.tensor.matmul(pa[s][:, 0:2 * D], lhsT=ablk[s][:, :], rhs=w2a[:, :], start=True, stop=False)
                nc.tensor.matmul(pa[s][:, 0:2 * D], lhsT=cblk[s][:, :], rhs=vec[:, :],
                                 start=False, stop=True).then_inc(node_mm, 1)

            def pre_products(i, j):
                pe.wait_ge(window_in[j], i * 16 + 16)
                pe.wait_ge(ohT_ready, i * NG + (j + 1))
                if not first(i):
                    pe.wait_ge(h_ready, i * NG + (j + 1 - NG))
                for c in range(GT):
                    mm = nc.tensor.matmul(pre[j][:, c * D:(c + 1) * D], lhsT=lhs[:, j, c * P:(c + 1) * P],
                                          rhs=win[:, j, :], start=True, stop=True)
                mm.then_inc(pre_done, 1)

            def turn_rows(j):
                pe.wait_ge(gath_in[j], 16 * GT)
                if j >= len(turned):
                    pe.wait_ge(rowsT_ready, j + 1 - len(turned))
                for c in range(GT):
                    mm = nc.tensor.matmul(turned[j % len(turned)][:, c * P:(c + 1) * P], lhsT=gath[:, j, c, :],
                                          rhs=ident[:, :], start=True, stop=True)
                mm.then_inc(turn_done, 1)

            def first_rows(j):
                pe.wait_ge(rowsT_ready, j + 1)
                for c in range(GT):
                    nc.tensor.matmul(pre[j][:, c * D:(c + 1) * D], lhsT=h[:, j, c, :], rhs=w1s[:, :],
                                     start=(c == 0), stop=False)

            def first_products(j):
                pe.wait_ge(window_in[j], 16)
                pe.wait_ge(ohT_ready, j + 1)
                for c in range(GT):
                    mm = nc.tensor.matmul(pre[j][:, c * D:(c + 1) * D], lhsT=lhs[:, j, c * P:(c + 1) * P],
                                          rhs=win[:, j, :], start=False, stop=(c == GT - 1))
                mm.then_inc(pre_done, 1)

            def agg_products(i, j):
                pe.wait_ge(oh_ready, i * NG + (j + 1))
                pe.wait_ge(h_ready, i * NG + (j + 1))
                if not (first(i) and j < SUMS):
                    pe.wait_ge(added, i * NG + (j + 1 - SUMS))
                for c in range(GT):
                    nc.tensor.matmul(pagg[j % SUMS][:, 0:WIN], lhsT=h[:, j, c, :], rhs=onehot[:, j, c, :],
                                     start=(c == 0), stop=(c == GT - 1))
                nc.tensor.matmul(pagg[j % SUMS][:, WIN:WIN + GT * WIN], lhsT=ones[:, :],
                                 rhs=onehot[:, j, :, :].rearrange("p c w -> p (c w)"),
                                 start=True, stop=True).then_inc(agg_done, 1)

            def body(i):
                for j in range(NG):
                    if near(i, j, -1):
                        agg_products(*near(i, j, -1))
                    if j == 0 and closed(i, 1) is not None:
                        node_agg(*in_turn(closed(i, 1)))
                    if near(i, j, 2) and not first(near(i, j, 2)[0]):
                        pre_products(*near(i, j, 2))
                    if j == 3 and closed(i) is not None:
                        node_x(*in_turn(closed(i)))

            with pe.If(bad_v == 0):
                pe.wait_ge(prep, PREP)
                for j in range(NG):
                    turn_rows(j)
                    if j == 1:
                        pe.wait_ge(pdst_sb, NCH)
                    if j > 0:
                        first_rows(j - 1)
                first_rows(NG - 1)
                for j in range(NG):
                    first_products(j)
                run_iterations(pe, body, {2: fold})
                node_x(*ENDING)
                agg_products(FINAL, NG - 1)
                node_agg(*in_turn(LAST - 1))
                node_agg(*ENDING)
            with pe.Else():
                pe.wait_ge(pdst_sb, NCH)
                fold()

                def sum_tile(t):
                    pe.wait_ge(g_ef, t * 16 + 16)
                    if not isinstance(t, int):
                        pe.wait_ge(g_sum, t)
                    nc.tensor.matmul(pre[0][:, 0:D], lhsT=sef[:, :], rhs=win[0:DE, 0, :],
                                     start=True, stop=True).then_inc(g_pre, 1)
                    pe.wait_ge(g_h, t + 1)
                    take_waits(pe)
                    with pe.Fori(0, NB) as b:
                        pe.wait_ge(g_oh, t * NB + b + 1)
                        nc.tensor.matmul(pagg[0][:, 0:P], lhsT=sh[:, :], rhs=soh[:, :], start=True, stop=True)
                        nc.tensor.matmul(pagg[0][:, P:2 * P], lhsT=ones[:, :], rhs=soh[:, :],
                                         start=True, stop=True).then_inc(g_mm, 1)
                sum_tile(0)
                with pe.Fori(1, NT) as t:
                    sum_tile(t)

                def stage(b):
                    node_x(*in_turn(b))
                    node_agg(*in_turn(b))
                loop_blocks(pe, stage)

        @block.vector
        def _(dve):
            def done(n):
                dve.wait_ge(prep, n)

            nc.vector.memset(ones[:, :], 1.0).then_inc(ones_ready, 1)
            nc.vector.memset(vec[:, :], 0.0).then_inc(vec_zero, 1)
            nc.vector.memset(aggcnt[:, GT, :], 0.0).then_inc(zero_ready, 1)
            dve.wait_ge(iota_ready, 2)
            nc.vector.tensor_copy(iota_f[:, :], iota_i[:, :]).then_inc(prep, 1)
            nc.vector.tensor_copy(node_f[:, :], node_i[:, :]).then_inc(prep, 1)
            dve.wait_ge(tab_in, 48)
            nc.vector.tensor_copy(base_f[:, :], base_i[:, :]).then_inc(prep, 1)
            nc.vector.tensor_copy(dst_f[:, :], dst_i[:, :]).then_inc(prep, 1)
            done(4)
            nc.vector.tensor_scalar(base_col[:, :], base_f[:, :], -1.0, node_f[:, 0:1], ALU.mult,
                                    ALU.add).then_inc(prep, 1)
            nc.vector.tensor_tensor(slack[:, :], base_f[:, :], open_i[:, :], ALU.subtract).then_inc(prep, 1)
            nc.vector.tensor_tensor(rel[:, :].rearrange("p (g t) -> p g t", t=GT),
                                    dst_f[:, :].rearrange("p (g t) -> p g t", t=GT),
                                    base_f[:, :].rearrange("p (g a) -> p g a", a=1).to_broadcast([P, NBASE, GT]),
                                    ALU.subtract).then_inc(prep, 1)
            done(7)
            nc.vector.tensor_reduce(red[:, 0:1], rel[:, :], AX.X, ALU.max).then_inc(prep, 1)
            nc.vector.tensor_reduce(red[:, 1:2], rel[:, :], AX.X, ALU.min).then_inc(prep, 1)
            nc.vector.tensor_reduce(red[:, 2:3], slack[:, :], AX.X, ALU.min).then_inc(prep, 1)
            done(10)
            nc.vector.tensor_scalar(bad[:, 0:1], red[:, 0:1], float(WIN), None, ALU.is_ge).then_inc(prep, 1)
            nc.vector.tensor_scalar(bad[:, 1:3], red[:, 1:3], 0.0, None, ALU.is_lt).then_inc(prep, 1)
            done(12)
            nc.vector.tensor_reduce(bad[:, 3:4], bad[:, 0:3], AX.X, ALU.add).then_inc(bad_ready, 1)
            nc.vector.tensor_scalar(ident[:, :], iota_f[:, :], node_f[:, 0:1], float(WIN), ALU.add,
                                    ALU.is_equal).then_inc(prep, 1)
            for n in range(2 * NCH):
                if n == NCH:
                    dve.wait_ge(bad_mm, 1)
                    nc.vector.tensor_copy(flag[:, :], pflag[0:1, 0:1]).then_inc(flag_ready, 1)
                    dve.wait_ge(b1_in, 16)
                lo, hi = n % NCH * XCH, min((n % NCH + 1) * XCH, NB)
                bk = banks[n % len(banks)][:, 0:(hi - lo) * D].rearrange("p (b f) -> p b f", f=D)
                dve.wait_ge(tab_mm, n + 1)
                if n < NCH:
                    nc.vector.tensor_copy(pst[:, 0, lo:hi, :], bk).then_inc(psrc_sb, 1)
                else:
                    b1v = b1_bc[:, :].rearrange("p (a f) -> p a f", a=1).to_broadcast([P, hi - lo, D])
                    nc.vector.tensor_tensor(pst[:, 1, lo:hi, :], bk, b1v, ALU.add).then_inc(pdst_sb, 1)
            dve.wait_ge(flag_ready, 1)
            bad_v = dve.value_load(flag[0:1, 0:1], min_val=0, max_val=3 * P)

            NEWTON = 3
            GUESS = 3
            STEPS = 2 * NEWTON
            AT_MIX = 1
            AT_MOM1 = AT_MIX + 3
            AT_GUESS1 = AT_MOM1 + 2
            AT_IN = AT_GUESS1 + GUESS + STEPS
            AT_MOM2 = AT_IN + 3
            AT_GUESS2 = AT_MOM2 + 2
            CHAIN = AT_GUESS2 + GUESS + STEPS

            def after(s, m, n):
                dve.wait_ge(chain[s], m * CHAIN + n)

            def count_rows(b, s, m):
                if not first(m):
                    dve.wait_ge(node_mm, b)
                nc.vector.tensor_reduce(cblk[s][:, :], aggcnt[0:VR, 1:1 + GT, bass.ds(b * P, P)]
                                        .rearrange("p c n -> p n c"), AX.X, ALU.add).then_inc(cnt_ready, 1)
                dve.wait_ge(cnt_ready, b + 1)
                nc.vector.tensor_scalar(cblk[s][VR - 1:VR, :], cblk[s][VR - 1:VR, :], 1.0, None,
                                        ALU.max).then_inc(cblk_ready, 1)

            def gate_sum(b, s, m):
                dve.wait_ge(node_mm, b + 1)
                nc.vector.reciprocal(rcp[s][:, :], pa[s][:, 2 * D:2 * D + 1]).then_inc(chain[s], 1)
                after(s, m, 1)
                dve.wait_ge(xg_ready, b + 1)
                if not first(m):
                    dve.wait_ge(th_ready, b)
                nc.vector.scalar_tensor_tensor(out=gt[s][:, :], in0=pa[s][:, 0:2 * D], scalar=rcp[s][:, :],
                                               in1=xg[s][:, :], op0=ALU.mult, op1=ALU.add).then_inc(gt_ready, 1)

            def rsqrt_guess(blocks, n):
                for b, s, m in blocks:
                    nc.vector.tensor_scalar(nt[s][:, 0:1], mv[s][:, 1:2], EPS, None, ALU.add).then_inc(chain[s], 1)
                for b, s, m in blocks:
                    after(s, m, n + 1)
                    nc.vector.tensor_scalar(nhv[s][:, :], nt[s][:, 0:1], -0.5, None, ALU.mult).then_inc(chain[s], 1)
                    nc.vector.tensor_scalar(yi[s][:, :], nt[s][:, 0:1].bitcast(I32), -0.5, float(0x5F3759DF),
                                            ALU.mult, ALU.add).then_inc(chain[s], 1)

            def rsqrt_steps(blocks, n):
                for step in range(NEWTON):
                    for b, s, m in blocks:
                        y = nt[s][:, 2:3] if step else yi[s][:, :].bitcast(F32)
                        after(s, m, n + 2 * step)
                        nc.vector.scalar_tensor_tensor(out=nt[s][:, 1:2], in0=y, scalar=y, in1=nhv[s][:, :],
                                                       op0=ALU.mult, op1=ALU.mult).then_inc(chain[s], 1)
                    for b, s, m in blocks:
                        y = nt[s][:, 2:3] if step else yi[s][:, :].bitcast(F32)
                        after(s, m, n + 1 + 2 * step)
                        nc.vector.scalar_tensor_tensor(out=nt[s][:, 2:3], in0=nt[s][:, 1:2], scalar=1.5, in1=y,
                                                       op0=ALU.add, op1=ALU.mult).then_inc(chain[s], 1)

            def moments(blocks, rows, n):
                for b, s, m in blocks:
                    after(s, m, n)
                    nc.vector.bn_stats(stats[s][:, :], rows[s][:, :]).then_inc(chain[s], 1)
                for b, s, m in blocks:
                    after(s, m, n + 1)
                    if not isinstance(b, int):
                        take_waits(dve)
                    nc.vector.bn_aggr(mv[s][:, :], stats[s][:, :]).then_inc(chain[s], 1)
                for b, s, m in blocks:
                    after(s, m, n + 2)

            def mix_in(blocks):
                for b, s, m in blocks:
                    dve.wait_ge(th_ready, b + 1)
                    dve.wait_ge(blk_in[s], m * 32 + 32)
                    if isinstance(b, int):
                        dve.wait_ge(bc_in, 32)
                    xv = x_all[:, bass.ds(b, 1), :].rearrange("p a f -> p (a f)")
                    nc.vector.tensor_tensor(diff[s][:, :], xv, th[s][:, D:2 * D], ALU.subtract).then_inc(chain[s], 1)
                    nc.vector.tensor_tensor(xb[s][:, :], xv, beta_bc[:, :], ALU.add).then_inc(chain[s], 1)
                for b, s, m in blocks:
                    after(s, m, AT_MIX + 1)
                    nc.vector.scalar_tensor_tensor(out=mix[s][:, :], in0=th[s][:, 0:D], scalar=1.0, in1=diff[s][:, :],
                                                   op0=ALU.add, op1=ALU.mult).then_inc(chain[s], 1)
                for b, s, m in blocks:
                    after(s, m, AT_MIX + 3)
                    nc.vector.scalar_tensor_tensor(out=upd[s][:, :], in0=mix[s][:, :], scalar=0.5,
                                                   in1=th[s][:, D:2 * D], op0=ALU.mult, op1=ALU.add).then_inc(upd_ready, 1)
                for b, s, m in blocks:
                    dve.wait_ge(upd_ready, b + 1)
                moments(blocks, upd, AT_MOM1)
                rsqrt_guess(blocks, AT_GUESS1)

            def norm_in(blocks):
                rsqrt_steps(blocks, AT_GUESS1 + GUESS)
                for b, s, m in blocks:
                    after(s, m, AT_IN)
                    nc.vector.tensor_scalar(nrm[s][:, :], upd[s][:, :], mv[s][:, 0:1], nt[s][:, 2:3], ALU.subtract,
                                            ALU.mult).then_inc(chain[s], 1)
                for b, s, m in blocks:
                    after(s, m, AT_IN + 1)
                    nc.vector.tensor_tensor(ynew[s][:, :], nrm[s][:, :], gamma_bc[:, :], ALU.mult).then_inc(chain[s], 1)
                for b, s, m in blocks:
                    after(s, m, AT_IN + 2)
                    nc.vector.tensor_tensor(ysum[s][:, :], ynew[s][:, :], xb[s][:, :], ALU.add).then_inc(chain[s], 1)

            def moments_out(blocks):
                moments(blocks, ysum, AT_MOM2)
                rsqrt_guess(blocks, AT_GUESS2)

            def norm_out(blocks):
                rsqrt_steps(blocks, AT_GUESS2 + GUESS)
                for b, s, m in blocks:
                    after(s, m, CHAIN)
                    if not first(m):
                        dve.wait_ge(out_done, b * 16)
                    nc.vector.tensor_scalar(oblk[s][:, :], ysum[s][:, :], mv[s][:, 0:1], nt[s][:, 2:3], ALU.subtract,
                                            ALU.mult).then_inc(out_ready, 1)

            def prepare(i, j):
                if not first(i):
                    dve.wait_ge(agg_done, i * NG + (j + 1 - NG))
                i0 = iota_f[:, 0:WIN].rearrange("p (a w) -> p a w", a=1).to_broadcast([P, GT, WIN])
                r0 = (rel[:, bass.ds(i * TILES + j * GT, GT)].rearrange("p (k a) -> p k a", a=1)
                      .to_broadcast([P, GT, WIN]))
                nc.vector.tensor_tensor(onehot[:, j, :, :], i0, r0, ALU.is_equal).then_inc(oh_ready, 1)

            def add_rows(i, j):
                dve.wait_ge(pre_done, i * NG + (j + 1))
                dve.wait_ge(gath_in[j], i * (16 * GT) + 16 * GT)
                z = pre[j][:, :].rearrange("p (c f) -> p c f", f=D)
                nc.vector.tensor_tensor(z, z, gath[:, j, :, :], ALU.add).then_inc(sum_done, 1)

            def add_window(i, j, base):
                dve.wait_ge(agg_done, i * NG + (j + 1))
                if not (first(i) and j == 0):
                    dve.wait_ge(added, i * NG + j)
                w = aggcnt[:, :, bass.ds(base, WIN)]
                nc.vector.tensor_tensor(w, w, pagg[j % SUMS][:, 0:(1 + GT) * WIN]
                                        .rearrange("p (a w) -> p a w", w=WIN), ALU.add).then_inc(added, 1)

            def body(i):
                for j in range(NG):
                    if not first(i):
                        add_rows(i, j)
                    back = near(i, j, -1)
                    if back:
                        base = load_base(dve, *back)
                    if near(i, j, 1):
                        prepare(*near(i, j, 1))
                    if back:
                        add_window(*back, base)
                    if j == CLOSE and closed(i) is not None:
                        dve.wait_ge(added, i * NG + CLOSE)
                        count_rows(*in_turn(closed(i)))
                    if j == 0 and closed(i, 2) is not None:
                        norm_out([in_turn(closed(i, 2))])
                    if j == 0 and closed(i, 1) is not None:
                        gate_sum(*in_turn(closed(i, 1)))
                    if j == 1 and closed(i, 1) is not None:
                        mix_in([in_turn(closed(i, 1))])
                    if j == 2 and closed(i, 1) is not None:
                        norm_in([in_turn(closed(i, 1))])
                    if j == 3 and closed(i, 1) is not None and not (isinstance(i, int) and i == FINAL):
                        moments_out([in_turn(closed(i, 1))])

            with dve.If(bad_v == 0):
                prepare(0, 0)
                for j in range(NG):
                    dve.wait_ge(turn_done, j + 1)
                    nc.vector.tensor_copy(h[:, j, :, :], turned[j % len(turned)][:, :]
                                          .rearrange("p (c f) -> p c f", f=D)).then_inc(rowsT_ready, 1)
                dve.wait_ge(zero_ready, 1 + GT)
                run_iterations(dve, body)
                moments_out([in_turn(LAST - 2)])
                add_window(FINAL, NG - 1, load_base(dve, FINAL, NG - 1))
                dve.wait_ge(added, ITERS * NG)
                count_rows(*ENDING)
                norm_out([in_turn(LAST - 2)])
                both = [in_turn(LAST - 1), ENDING]
                for one in both:
                    gate_sum(*one)
                mix_in(both)
                norm_in(both)
                moments_out(both)
                norm_out(both)
            with dve.Else():
                def sum_tile(t):
                    dve.wait_ge(g_pre, t + 1)
                    dve.wait_ge(g_gath, t * 32 + 32)
                    if not isinstance(t, int):
                        dve.wait_ge(g_h, t)
                    nc.vector.tensor_tensor(pre[1][:, 0:D], pre[0][:, 0:D], sgath[:, 0, :], ALU.add).then_inc(g_sum0, 1)
                    dve.wait_ge(g_sum0, t + 1)
                    nc.vector.tensor_tensor(pre[1][:, 0:D], pre[1][:, 0:D], sgath[:, 1, :], ALU.add).then_inc(g_sum, 1)
                    if not isinstance(t, int):
                        dve.wait_ge(g_oh, t * NB)
                    nc.vector.tensor_copy(shift[:, :], dst_f[:, bass.ds(t, 1)]).then_inc(g_shift, 1)
                    with dve.Fori(0, NB) as b:
                        dve.wait_ge(g_shift, t * (NB + 1) + b + 1)
                        nc.vector.tensor_scalar(soh[:, :], iota_f[:, :], shift[:, 0:1], None,
                                                ALU.is_equal).then_inc(g_oh, 1)
                        dve.wait_ge(g_oh, t * NB + b + 1)
                        nc.vector.tensor_scalar(shift[:, :], shift[:, :], float(P), None,
                                                ALU.subtract).then_inc(g_shift, 1)
                        dve.wait_ge(g_mm, t * NB + b + 1)
                        w = aggcnt[:, 0:2, bass.ds(b * P, P)]
                        nc.vector.tensor_tensor(w, w, pagg[0][:, 0:2 * P].rearrange("p (a w) -> p a w", a=2),
                                                ALU.add).then_inc(g_added, 1)
                    dve.wait_ge(g_added, t * NB + NB)
                dve.wait_ge(zero_ready, 1 + GT)
                sum_tile(0)
                with dve.Fori(1, NT) as t:
                    sum_tile(t)

                def stage(b):
                    for step in (count_rows, gate_sum):
                        step(*in_turn(b))
                    for step in (mix_in, norm_in, moments_out, norm_out):
                        step([in_turn(b)])
                loop_blocks(dve, stage)


def kernel(x, src, dst, edge_attr_64, L0_gnn_W1, L0_gnn_b1, L0_gnn_W2, L0_gnn_b2, L0_gnn_Wg, L0_gnn_bg,
           L0_gnn_Wt, L0_gnn_bt, L0_gnn_gamma, L0_gnn_beta):
    import concourse.bacc as _bacc
    from concourse.bass_utils import run_bass_kernel_spmd as _run

    x, src, dst, ef = (np.asarray(a) for a in (x, src, dst, edge_attr_64))
    n, e = x.shape[0], src.shape[0]
    nb, nt, iters = shapes(n, e)
    src_p = np.concatenate([src, np.zeros(nt * P - e, src.dtype)])
    dst_p = np.concatenate([dst, np.full(nt * P - e, n, dst.dtype)])
    x_p = np.concatenate([x, np.zeros((nb * P - n, D), x.dtype)])
    ef_p = np.concatenate([ef, np.zeros((nt * P - e, DE), ef.dtype)])
    opened = np.array([[P * max(i - LAG + (j >= CLOSE), 0) for j in range(NG)] for i in range(iters)], np.int32)
    arrays = {
        "x": x_p, "xT": x_p.T, "src_pt": src_p.reshape(-1, P).T, "dst_pt": dst_p.reshape(nt, P).T,
        "dst_flat": dst_p.reshape(1, -1), "base_tab": dst_p[::GT * P].reshape(1, -1),
        "open_tab": opened.reshape(1, -1), "efT": ef_p.T,
        "W1": L0_gnn_W1, "b1": np.asarray(L0_gnn_b1).reshape(1, -1), "W2T": np.asarray(L0_gnn_W2).T,
        "b2": np.asarray(L0_gnn_b2).reshape(-1, 1), "Wg": L0_gnn_Wg, "bg": np.asarray(L0_gnn_bg).reshape(1, -1),
        "Wt": L0_gnn_Wt, "bt": np.asarray(L0_gnn_bt).reshape(1, -1),
        "gamma": np.asarray(L0_gnn_gamma).reshape(1, -1), "beta": np.asarray(L0_gnn_beta).reshape(1, -1),
    }
    arrays = {f"in_{k}": np.ascontiguousarray(v) for k, v in arrays.items()}
    nc = _bacc.Bacc("TRN2", target_bir_lowering=False, num_devices=1)
    args = [nc.dram_tensor(k, v.shape, mybir.dt.from_np(v.dtype), kind="ExternalInput").ap() for k, v in arrays.items()]
    out = nc.dram_tensor("out_x", (n, D), F32, kind="ExternalOutput").ap()
    gnn_kernel(nc, *args, out)
    r = _run(nc, [arrays], core_ids=[0])
    return r.results[0]["out_x"]
```
